# Optimizing a Trainium2 kernel written in Bass

```python
import numpy as np
import jax
import jax.numpy as jnp

def _softmax(x, axis=-1):
    return jax.nn.softmax(x, axis=axis)

def _gelu(x):
    return jax.nn.gelu(x, approximate=True)

def _silu(x):
    return jax.nn.silu(x)

def _sigmoid(x):
    return jax.nn.sigmoid(x)

def _layernorm(x, axis=-1, eps=1e-05):
    m = jnp.mean(x, axis=axis, keepdims=True)
    v = jnp.var(x, axis=axis, keepdims=True)
    return (x - m) / jnp.sqrt(v + eps)

def _scatter_add(tgt, idx, src, axis=0):
    return tgt.at[idx].add(src)

def _segment_sum(src, seg, n):
    return jax.ops.segment_sum(src, seg, n)
kernel_name = 'mk_gnn_preln_d2_gnn_r32_520514'

def setup_inputs(seed: int=0):
    np.random.seed(seed)
    _w = jnp.asarray

    def _rec_inputs():
        import jax
        import jax.numpy as jnp
        _gk = jax.random.key(seed)
        x = -0.0003713 + 1 * jax.random.normal(jax.random.fold_in(_gk, 1), (50000, 256), jnp.float32)
        src = jax.random.randint(jax.random.fold_in(_gk, 2), (25000,), 0, 50000, jnp.int32)
        dst = jax.random.randint(jax.random.fold_in(_gk, 3), (25000,), 0, 50000, jnp.int32)
        _o = jnp.argsort(dst, stable=True)
        src = src[_o]
        dst = dst[_o]
        edge_weight = jax.random.uniform(jax.random.fold_in(_gk, 13), (25000,), jnp.float32, 0.0, 0.0312499)
        return (x, src, dst, edge_weight)
    x, src, dst, edge_weight = _rec_inputs()

    def _L0_gnn_setup():
        import jax, jax.numpy as jnp
        import numpy as np
        N = 50000
        E = 50000
        D_IN = 256
        D_OUT = 256
        key = jax.random.key(seed)
        k1, k2, k3, k4, k5 = jax.random.split(key, 5)
        x = jax.random.normal(k1, (N, D_IN), dtype=jnp.float32)
        stdv = 1.0 / np.sqrt(D_IN)
        W = jax.random.normal(k2, (D_OUT, D_IN), dtype=jnp.float32) * stdv
        edge_row = jax.random.randint(k3, (E,), 0, N, dtype=jnp.int32)
        edge_col = jax.random.randint(k4, (E,), 0, N, dtype=jnp.int32)
        edge_val = jax.random.uniform(k5, (E,), dtype=jnp.float32) / 32.0
        return {'x': x, 'W': W, 'edge_row': edge_row, 'edge_col': edge_col, 'edge_val': edge_val}
    _L0_gnn_all = _L0_gnn_setup()
    _L0_gnn_in = {k: v for k, v in _L0_gnn_all.items() if k in ('W',)}
    del _L0_gnn_all

    def _L1_gnn_setup():
        import jax, jax.numpy as jnp
        import numpy as np
        N_NODES = 3125
        N_EDGES = 10000
        D_IN, D_HID, D_OUT = (256, 1024, 256)
        BN_EPS = 1e-05
        key = jax.random.key(seed)
        ks = jax.random.split(key, 6)
        x = jax.random.normal(ks[0], (N_NODES, D_IN), dtype=jnp.float32)
        edge_index = jax.random.randint(ks[1], (2, N_EDGES), 0, N_NODES, dtype=jnp.int64)
        W1 = jax.random.normal(ks[2], (D_IN, D_HID), dtype=jnp.float32) * (1.0 / np.sqrt(D_IN))
        b1 = jnp.zeros((D_HID,), dtype=jnp.float32)
        gamma = jnp.ones((D_HID,), dtype=jnp.float32)
        beta = jnp.zeros((D_HID,), dtype=jnp.float32)
        W2 = jax.random.normal(ks[3], (D_HID, D_OUT), dtype=jnp.float32) * (1.0 / np.sqrt(D_HID))
        b2 = jnp.zeros((D_OUT,), dtype=jnp.float32)
        return {'x': x, 'edge_index': edge_index, 'W1': W1, 'b1': b1, 'gamma': gamma, 'beta': beta, 'W2': W2, 'b2': b2}
    _L1_gnn_all = _L1_gnn_setup()
    _L1_gnn_in = {k: v for k, v in _L1_gnn_all.items() if k in ('W1', 'b1', 'gamma', 'beta', 'W2', 'b2')}
    del _L1_gnn_all
    return {'x': x, 'src': src, 'dst': dst, 'edge_weight': edge_weight, 'L0_gnn_W': _L0_gnn_in['W'], 'L1_gnn_W1': _L1_gnn_in['W1'], 'L1_gnn_b1': _L1_gnn_in['b1'], 'L1_gnn_gamma': _L1_gnn_in['gamma'], 'L1_gnn_beta': _L1_gnn_in['beta'], 'L1_gnn_W2': _L1_gnn_in['W2'], 'L1_gnn_b2': _L1_gnn_in['b2']}

def reference(x, src, dst, edge_weight, L0_gnn_W, L1_gnn_W1, L1_gnn_b1, L1_gnn_gamma, L1_gnn_beta, L1_gnn_W2, L1_gnn_b2):
    import jax
    import jax.numpy as jnp

    def _L0_gnn_ref(x, W, edge_row, edge_col, edge_val):
        import jax, jax.numpy as jnp
        import numpy as np
        N = 50000
        E = 50000
        D_IN = 256
        D_OUT = 256
        support = jnp.einsum('ni,oi->no', x, W)
        msgs = support[edge_col] * edge_val[:, None]
        output = jax.ops.segment_sum(msgs, edge_row, num_segments=N)
        return output

    def _L1_gnn_ref(x, edge_index, W1, b1, gamma, beta, W2, b2):
        import jax, jax.numpy as jnp
        import numpy as np
        N_NODES = 3125
        N_EDGES = 10000
        D_IN, D_HID, D_OUT = (256, 1024, 256)
        BN_EPS = 1e-05
        src, dst = (edge_index[0], edge_index[1])
        agg = jax.ops.segment_sum(x[src], dst, num_segments=x.shape[0])
        h = agg + x
        h1 = h @ W1 + b1
        mean = jnp.mean(h1, axis=0)
        var = jnp.mean(jnp.square(h1 - mean), axis=0)
        h1 = (h1 - mean) * jax.lax.rsqrt(var + BN_EPS) * gamma + beta
        h1 = jax.nn.relu(h1)
        out = jax.nn.relu(h1 @ W2 + b2)
        return out
    edge_index = jnp.stack([src, dst])
    h = jnp.maximum(_layernorm(x, axis=-1), 0.0)
    x = x + _L0_gnn_ref(h, L0_gnn_W, src, dst, edge_weight)
    h = jnp.maximum(_layernorm(x, axis=-1), 0.0)
    x = x + _L1_gnn_ref(h, edge_index, L1_gnn_W1, L1_gnn_b1, L1_gnn_gamma, L1_gnn_beta, L1_gnn_W2, L1_gnn_b2)
    return x

_drawn_inputs = setup_inputs


def setup_inputs(seed=0):
    import zlib

    import numpy as np

    out = dict(_drawn_inputs(seed))
    spreads = {'L1_gnn_b1': (0.0, 0.8),
     'L1_gnn_gamma': (1.0, 0.2),
     'L1_gnn_beta': (0.0, 0.1),
     'L1_gnn_b2': (0.0, 0.1)}
    factors = {'edge_weight': 8.0, 'L0_gnn_W': 5.058}
    for name, (base, spread) in spreads.items():
        noise = np.random.default_rng([zlib.crc32(name.encode()), seed]).standard_normal(out[name].shape)
        drawn = base * np.exp(spread * noise) if base else spread * noise
        out[name] = jnp.asarray(drawn.astype(out[name].dtype))
    for name, factor in factors.items():
        out[name] = (out[name] * factor).astype(out[name].dtype)
    return out
```

```python
def gnn_program(nc, x, src, dst, edge_weight, W, W1, b1, gamma, beta, W2, b2, out):
    from contextlib import ExitStack

    import concourse.bass as bass
    from concourse import mybir

    F32, F32R, I32 = mybir.dt.float32, mybir.dt.float32r, mybir.dt.int32
    ALU = mybir.AluOpType
    ACT = mybir.ActivationFunctionType

    P = 128
    N, D = x.shape
    E = src.shape[0]
    HID = W1.shape[1]
    KB = D // P
    MB = HID // P
    EPS = 1e-5

    PAIR = 2
    COLS = -(-E // (P * PAIR)) * PAIR
    GROUPS = COLS // PAIR
    FULL_EDGE_ROWS = E // COLS
    LAST_EDGES = E - FULL_EDGE_ROWS * COLS
    assert GROUPS % 2 == 0 and FULL_EDGE_ROWS == P - 1
    DUMP_ROWS = P * PAIR

    ROWS = 4
    CHUNK = P * ROWS
    FULL_CHUNKS = N // CHUNK
    TAIL_NODES = N - FULL_CHUNKS * CHUNK
    TAIL_ROWS = 3
    TAIL_P = TAIL_NODES // TAIL_ROWS
    assert TAIL_P * TAIL_ROWS == TAIL_NODES and TAIL_P <= P and TAIL_P % 16 == 0
    CHUNKS = FULL_CHUNKS + 1
    assert CHUNKS == GROUPS

    ZERO_PIECES = 50
    ZERO_P = 80
    ZERO_LEN = N * D // ZERO_PIECES // ZERO_P
    assert ZERO_PIECES * ZERO_P * ZERO_LEN == N * D and ZERO_LEN >= DUMP_ROWS * D // P
    COPY_PIECES = 4
    COPY_ROWS = 500
    assert N % (COPY_PIECES * COPY_ROWS) == 0

    x1_table = nc.dram_tensor("x1_table", (N + DUMP_ROWS, D), F32, kind="Internal").ap()
    agg_table = nc.dram_tensor("agg_table", (N + DUMP_ROWS, D), F32, kind="Internal").ap()

    def full_chunks(table):
        return table[0:FULL_CHUNKS * CHUNK, :].rearrange("(c p j) d -> c p (j d)", p=P, j=ROWS)

    def tail_chunk(table):
        return table[FULL_CHUNKS * CHUNK:N, :].rearrange("(p j) d -> p (j d)", j=TAIL_ROWS)

    with ExitStack() as ctx:
        def sb(name, shape, dt=F32):
            return ctx.enter_context(nc.sbuf_tensor(name, shape, dt))

        def sem(name):
            return ctx.enter_context(nc.semaphore(name))

        ident = sb("ident", [P, P])
        ones = sb("ones", [P, P])
        ones_r = sb("ones_r", [P, P], F32R)
        zeros = sb("zeros", [P, ZERO_LEN])
        earlier = sb("earlier", [P, PAIR, PAIR * P])
        gather_ids = [sb(f"gather_ids{i}", [P, COLS], I32) for i in range(2)]
        target_ids = [sb(f"target_ids{i}", [P, COLS], I32) for i in range(2)]
        dump_ids = sb("dump_ids", [P, COLS], I32)
        weights = sb("weights", [P, COLS])
        edge_info = [sb(f"edge_info{i}", [P, GROUPS, 3 * PAIR]) for i in range(2)]
        info_now = [sb(f"info_now{s}", [P, 3 * PAIR]) for s in range(2)]
        gather_now = [sb(f"gather_now{s}", [P, PAIR], I32) for s in range(2)]
        scatter_now = [sb(f"scatter_now{s}", [P, PAIR], I32) for s in range(2)]
        gathered_rows = [sb(f"gathered_rows{s}", [P, PAIR, D]) for s in range(2)]
        row_norm = [sb(f"row_norm{s}", [P, 2, PAIR]) for s in range(2)]
        row_stats = sb("row_stats", [P, PAIR, 6])
        row_moments = [sb(f"row_moments{s}", [P, PAIR, 2]) for s in range(2)]
        row_std = [sb(f"row_std{s}", [P, PAIR]) for s in range(2)]
        eps_col = sb("eps_col", [P, 1])
        normed = [sb(f"normed{s}", [P, PAIR, D]) for s in range(2)]
        same = [sb(f"same{s}", [P, PAIR, PAIR * P]) for s in range(2)]
        same_earlier = sb("same_earlier", [P, PAIR, PAIR * P])
        n_earlier = sb("n_earlier", [P, PAIR])
        shift = sb("shift", [P, PAIR])
        summedT = [sb(f"summedT{s}", [P, KB, PAIR * P]) for s in range(2)]
        message = [sb(f"message{s}", [P, PAIR, D]) for s in range(2)]
        x1_in = [sb(f"x1_in{s}", [P, ROWS, D]) for s in range(2)]
        agg_in = [sb(f"agg_in{s}", [P, ROWS, D]) for s in range(2)]
        node_stats = sb("node_stats", [P, ROWS, 6])
        chunk_moments = sb("chunk_moments", [P, ROWS, 2])
        node_moments = sb("node_moments", [P, CHUNKS, ROWS, 2])
        node_rstd = sb("node_rstd", [P, CHUNKS, ROWS])
        node_std = sb("node_std", [P, CHUNKS, ROWS])
        node_shift = sb("node_shift", [P, CHUNKS, ROWS])
        norm_now = [sb(f"norm_now{s}", [P, 2, ROWS]) for s in range(2)]
        relu_ln = sb("relu_ln", [P, ROWS, D])
        h = sb("h", [P, ROWS, D])
        gram_in = [sb(f"gram_in{s}", [P, ROWS, 2, D], F32R) for s in range(2)]
        w_rows = sb("w_rows", [P, KB, D])
        wT = sb("wT", [P, KB, D])
        w1_f = sb("w1_f", [P, KB, HID])
        w1_hi = sb("w1_hi", [P, KB, HID], F32R)
        w1_lo = sb("w1_lo", [P, KB, HID], F32R)
        w2_f = sb("w2_f", [P, MB, D])
        w2_hl = sb("w2_hl", [P, MB, 2, D], F32R)
        b2_bc = sb("b2_bc", [P, D])
        hid_vec = sb("hid_vec", [P, 3, MB])
        b1_v, gamma_v, beta_v = (hid_vec[:, i, :] for i in range(3))
        gram0 = sb("gram0", [P, 2 * D])
        gram_sum = sb("gram_sum", [P, D])
        gram1 = sb("gram1", [P, D + P])
        mu_row = sb("mu_row", [P, D])
        mu_col = sb("mu_col", [P, KB])
        cov = [sb(f"cov{k}", [P, D]) for k in range(KB)]
        w1_cov = sb("w1_cov", [P, KB, HID])
        bn_scale = sb("bn_scale", [P, MB])
        bn_std = sb("bn_std", [P, MB])
        bn_bias = sb("bn_bias", [P, MB])
        bn_mean = sb("bn_mean", [P, MB])
        hT_hi = sb("hT_hi", [P, KB, CHUNK], F32R)
        hT_lo = sb("hT_lo", [P, KB, CHUNK], F32R)
        hid = [sb(f"hid{i}", [P, CHUNK]) for i in range(2)]
        hid_hi = [sb(f"hid_hi{i}", [P, CHUNK], F32R) for i in range(4)]
        hid_lo = [sb(f"hid_lo{i}", [P, CHUNK], F32R) for i in range(4)]
        out_sb = [sb(f"out_sb{s}", [P, ROWS, D]) for s in range(2)]

        ps_a = ctx.enter_context(nc.psum_tensor("ps_a", [P, 4, 512], F32))
        ps_b = ctx.enter_context(nc.psum_tensor("ps_b", [P, 4, 512], F32))

        ids_blank = sem("ids_blank")
        consts_ready = sem("consts_ready")
        ids_loaded = sem("ids_loaded")
        w_loaded = sem("w_loaded")
        w12_loaded = sem("w12_loaded")
        x1_copied = sem("x1_copied")
        dump_zeroed = sem("dump_zeroed")
        agg_zeroed = sem("agg_zeroed")
        info_built = sem("info_built")
        wT_done = sem("wT_done")
        wT_ready = sem("wT_ready")
        dve_step = sem("dve_step")
        pool_gate = sem("pool_gate")

        class Layer:
            def __init__(self, n):
                self.n = n
                self.gather_from = (x, x1_table)[n]
                self.scatter_to = (x1_table, agg_table)[n]
                self.gather_ids = gather_ids[1 - n]
                self.info = edge_info[n]
                self.info_ready = sem(f"info_ready_L{n}")
                self.gather_ready = sem(f"gather_ready_L{n}")
                self.gathered = [sem(f"gathered_L{n}_{s}") for s in range(2)]
                self.moments_ready = sem(f"moments_ready_L{n}")
                self.std_ready = sem(f"std_ready_L{n}")
                self.norm_ready = sem(f"norm_ready_L{n}")
                self.normed_ready = sem(f"normed_ready_L{n}")
                self.targets_spread = sem(f"targets_spread_L{n}")
                self.same_ready = sem(f"same_ready_L{n}")
                self.scatter_ready = sem(f"scatter_ready_L{n}")
                self.summed = sem(f"summed_L{n}")
                self.summed_out = sem(f"summed_out_L{n}")
                self.message_done = sem(f"message_done_L{n}")
                self.message_ready = sem(f"message_ready_L{n}")
                self.scattered = [sem(f"scattered_L{n}_{s}") for s in range(2)]
                self.retired = sem(f"retired_L{n}")

        layers = [Layer(0), Layer(1)]

        stats_loaded = [sem(f"stats_loaded{s}") for s in range(2)]
        stats_taken = sem("stats_taken")
        stats_done = sem("stats_done")
        node_std_ready = sem("node_std_ready")
        gram_x_loaded = [sem(f"gram_x_loaded{s}") for s in range(2)]
        gram_a_loaded = [sem(f"gram_a_loaded{s}") for s in range(2)]
        norm_picked = sem("norm_picked")
        gram_relu = sem("gram_relu")
        gram_h = sem("gram_h")
        gram_hi = sem("gram_hi")
        gram_lo = sem("gram_lo")
        gram_used = sem("gram_used")
        bn_pe = sem("bn_pe")
        bn_act = sem("bn_act")
        bn_ready = sem("bn_ready")
        w12_split = sem("w12_split")

        main_loaded = [sem(f"main_loaded{s}") for s in range(2)]
        ln_ready = sem("ln_ready")
        h_ready = sem("h_ready")
        hT_done = sem("hT_done")
        hT_hi_ready = sem("hT_hi_ready")
        hT_lo_ready = sem("hT_lo_ready")
        up_done = sem("up_done")
        hid_ready = sem("hid_ready")
        hid_hi_ready = sem("hid_hi_ready")
        hid_lo_ready = sem("hid_lo_ready")
        down_done = sem("down_done")
        down_read = sem("down_read")
        out_ready = sem("out_ready")
        out_stored = [sem(f"out_stored{s}") for s in range(2)]
        out_retired = sem("out_retired")

        block = ctx.enter_context(nc.Block())

        MAIN_PAIRS = (CHUNKS - 4) // 2
        assert CHUNKS == 4 + 2 * MAIN_PAIRS

        def shape_of(n):
            return (TAIL_P, TAIL_ROWS) if isinstance(n, int) and n == CHUNKS - 1 else (P, ROWS)

        def main_schedule(eng, step):
            step(0, 0, 0)
            with eng.Fori(0, MAIN_PAIRS) as i:
                step(2 * i + 1, 1, i)
                step(2 * i + 2, 0, i + 1)
            for n in range(CHUNKS - 3, CHUNKS):
                step(n, n % 2, n // 2)

        def chunk_schedule(eng, step):
            with eng.Fori(0, FULL_CHUNKS // 2) as i:
                step(2 * i, 0, i)
                step(2 * i + 1, 1, i)
            for c in range(FULL_CHUNKS // 2 * 2, CHUNKS):
                step(c, c % 2, c // 2)

        def chunk_of(table, c):
            if isinstance(c, int) and c == CHUNKS - 1:
                return tail_chunk(table)
            return full_chunks(table)[bass.ds(c, 1), :, :].rearrange("c p e -> p (c e)")

        def tile_of(tile, c):
            p, j = shape_of(c)
            return tile[0:p, 0:j, :].rearrange("p j d -> p (j d)")

        @block.sync
        def _(sp):
            sp.sem_inc(out_retired, 2)
            sp.wait_ge(ids_blank, 1)
            def load_edges(tile, ids):
                sp.dma_start(tile[0:FULL_EDGE_ROWS, :],
                             ids[0:FULL_EDGE_ROWS * COLS].rearrange("(p c) -> p c", c=COLS)).then_inc(ids_loaded, 16)
                sp.dma_start(tile[FULL_EDGE_ROWS:P, 0:LAST_EDGES],
                             ids[FULL_EDGE_ROWS * COLS:E].rearrange("(p c) -> p c", p=1)).then_inc(ids_loaded, 16)
            for i, ids in ((1, dst), (0, src)):
                load_edges(gather_ids[i], ids)
                load_edges(target_ids[i], ids)
            load_edges(weights, edge_weight)
            sp.dma_start(w_rows[:, :, :], W.rearrange("(b p) i -> p b i", p=P)).then_inc(w_loaded, 16)
            for i in range(COPY_PIECES):
                rows = N // COPY_PIECES
                a = x[i * rows:(i + 1) * rows, :].rearrange("(a b) d -> a (b d)", b=rows // COPY_ROWS)
                b = x1_table[i * rows:(i + 1) * rows, :].rearrange("(a b) d -> a (b d)", b=rows // COPY_ROWS)
                sp.dma_start(b, a).then_inc(x1_copied, 16)
            sp.dma_start(w1_f[:, :, :], W1.rearrange("(k p) n -> p k n", p=P)).then_inc(w12_loaded, 16)
            sp.dma_start(w2_f[:, :, :], W2.rearrange("(m p) n -> p m n", p=P)).then_inc(w12_loaded, 16)
            sp.dma_start(b2_bc[:, :], b2.rearrange("(a n) -> a n", a=1).to_broadcast([P, D])).then_inc(w12_loaded, 16)
            with nc.allow_non_contiguous_dma(reason="three vectors of HID values, once"):
                for i, v in enumerate((b1, gamma, beta)):
                    sp.dma_start(hid_vec[:, i, :], v.rearrange("(m p) -> p m", p=P)).then_inc(w12_loaded, 16)
            sp.wait_ge(consts_ready, 1)
            for table in (x1_table, agg_table):
                sp.dma_start(table[N:N + DUMP_ROWS, :].rearrange("(p j) d -> p (j d)", p=P),
                             zeros[:, 0:PAIR * D]).then_inc(dump_zeroed, 16)
            agg_pieces = agg_table[0:N, :].rearrange("n d -> (n d)").rearrange("(i p e) -> i p e", i=ZERO_PIECES, p=ZERO_P)
            with sp.Fori(0, ZERO_PIECES) as i:
                sp.wait_ge(layers[0].normed_ready, i + 1)
                sp.dma_start(agg_pieces[bass.ds(i, 1), :, :].rearrange("i p e -> p (i e)"),
                             zeros[0:ZERO_P, :]).then_inc(agg_zeroed, 16)

            sp.wait_ge(layers[0].retired, GROUPS + 2)

            def load_stats(c, s, k):
                sp.wait_ge(stats_taken, c + 1)
                sp.dma_start(tile_of(x1_in[s], c), chunk_of(x1_table, c)).then_inc(stats_loaded[s], 16)
            chunk_schedule(sp, load_stats)

            sp.wait_ge(stats_taken, CHUNKS + 2)
            sp.wait_ge(layers[1].retired, GROUPS + 2)

            def load_gram(c, s, k):
                sp.wait_ge(gram_h, c + 1)
                sp.dma_start(tile_of(x1_in[s], c), chunk_of(x1_table, c)).then_inc(gram_x_loaded[s], 16)
                sp.dma_start(tile_of(agg_in[s], c), chunk_of(agg_table, c)).then_inc(gram_a_loaded[s], 16)
            chunk_schedule(sp, load_gram)
            sp.wait_ge(gram_h, CHUNKS + 2)

            def load_main(n, s):
                sp.dma_start(tile_of(x1_in[s], n), chunk_of(x1_table, n)).then_inc(main_loaded[s], 16)
                sp.dma_start(tile_of(agg_in[s], n), chunk_of(agg_table, n)).then_inc(main_loaded[s], 16)

            def store(n, s):
                sp.dma_start(chunk_of(out, n), tile_of(out_sb[s], n)).then_inc(out_stored[s], 16)

            load_main(0, 0)
            load_main(1, 1)
            def load_and_store(n, s, k):
                sp.wait_ge(out_ready, n + 1)
                load_main(n + 2, s)
                store(n, s)
                sp.wait_ge(out_stored[s], 16 * k + 16)
                sp.sem_inc(out_retired, 1)
            with sp.Fori(0, (CHUNKS - 4) // 2) as i:
                load_and_store(2 * i, 0, i)
                load_and_store(2 * i + 1, 1, i)
            load_and_store(CHUNKS - 4, 0, (CHUNKS - 4) // 2)
            load_and_store(CHUNKS - 3, 1, (CHUNKS - 4) // 2)
            for n in (CHUNKS - 2, CHUNKS - 1):
                sp.wait_ge(out_ready, n + 1)
                store(n, n % 2)
            for s in range(2):
                sp.wait_ge(out_stored[s], 16 * (CHUNKS // 2))

        @block.gpsimd
        def _(pool):
            dump_pattern = [[0, GROUPS], [1, PAIR]]
            for t in (dump_ids, target_ids[0], target_ids[1]):
                pool.iota(t[:, :], pattern=dump_pattern, base=N, channel_multiplier=PAIR)
            pool.memset(gather_ids[0][:, :], 0)
            pool.memset(gather_ids[1][:, :], 0)
            pool.memset(weights[:, :], 0.0).then_inc(ids_blank, 1)
            pool.memset(zeros[:, :], 0.0).then_inc(consts_ready, 1)
            pool.memset(node_moments[:, :, :, :], 1.0)
            pool.memset(eps_col[:, :], EPS)
            pool.memset(ident[:, :], 0.0)
            pool.memset(earlier[:, :, :], 0.0)
            pool.memset(ones[:, :], 1.0).then_inc(consts_ready, 1)
            pool.wait_ge(consts_ready, 2)
            pool.affine_select(out=ident[:, :], in_=ident[:, :], compare_op=ALU.not_equal, fill=1.0,
                               base=0, pattern=[[-1, P]], channel_multiplier=1)
            pool.tensor_copy(earlier[:, 1, 0:P], ones[:, :])
            pool.affine_select(out=earlier[:, 0, 0:P], in_=ones[:, :], compare_op=ALU.is_gt, fill=0.0,
                               base=0, pattern=[[-1, P]], channel_multiplier=1)
            pool.affine_select(out=earlier[:, 1, P:2 * P], in_=ones[:, :], compare_op=ALU.is_gt, fill=0.0,
                               base=0, pattern=[[-1, P]], channel_multiplier=1).then_inc(consts_ready, 1)
            for l in layers:
                pool.sem_inc(l.retired, 2)

            def gather(l, s):
                for a in range(PAIR):
                    pool.indirect_dma_start(gathered_rows[s][:, a, :], None, l.gather_from,
                                            bass.IndirectOffsetOnAxis(ap=gather_now[s][:, a:a + 1], axis=0)
                                            ).then_inc(l.gathered[s], 16)

            def scatter(l, s):
                for a in range(PAIR):
                    pool.indirect_dma_start(l.scatter_to,
                                            bass.IndirectOffsetOnAxis(ap=scatter_now[s][:, a:a + 1], axis=0),
                                            message[s][:, a, :], None, compute_op=ALU.add
                                            ).then_inc(l.scattered[s], 16)

            def step(l, g, s, k, more):
                pool.wait_ge(l.scatter_ready, g + 1)
                pool.wait_ge(l.message_ready, g + 3)
                pool.sem_inc(pool_gate, 1)
                scatter(l, s)
                if more:
                    pool.wait_ge(l.gather_ready, g + 3)
                    pool.wait_ge(l.normed_ready, g + 1)
                    pool.sem_inc(pool_gate, 1)
                    gather(l, s)
                pool.wait_ge(l.scattered[s], 16 * PAIR * (k + 1))
                pool.sem_inc(l.retired, 1)

            for l in layers:
                for s in range(2):
                    pool.wait_ge(l.gather_ready, s + 1)
                    gather(l, s)
                if l.n == 0:
                    pool.wait_ge(x1_copied, 16 * COPY_PIECES)
                    pool.wait_ge(dump_zeroed, 32)
                else:
                    pool.wait_ge(agg_zeroed, 16 * ZERO_PIECES)
                with pool.Fori(0, GROUPS // 2 - 1) as i:
                    step(l, 2 * i, 0, i, True)
                    step(l, 2 * i + 1, 1, i, True)
                for g in (GROUPS - 2, GROUPS - 1):
                    step(l, g, g % 2, g // 2, False)

        @block.scalar
        def _(act):
            act.wait_ge(wT_done, 1)
            act.activation(wT[:, :, :].rearrange("p k o -> p (k o)"), ps_a[:, 0, 0:KB * D], ACT.Copy).then_inc(wT_ready, 1)

            def step(l, g, s, k):
                act.wait_ge(l.moments_ready, g + 1)
                act.activation(row_std[s][:, :], row_moments[s][:, :, 1], ACT.Sqrt, bias=eps_col[:, :]).then_inc(l.std_ready, 1)
                act.wait_ge(l.norm_ready, g + 1)
                act.wait_ge(l.summed if l.n == 0 else l.message_done, g + 1)
                for a in range(PAIR):
                    ins = act.activation(normed[s][:, a, :], gathered_rows[s][:, a, :], ACT.Relu,
                                         scale=row_norm[s][:, 0, a:a + 1], bias=row_norm[s][:, 1, a:a + 1])
                ins.then_inc(l.normed_ready, 1)
                if l.n == 0:
                    act.wait_ge(l.summed, g + 3)
                    act.activation(summedT[s][:, :, :].rearrange("p k q -> p (k q)"), ps_a[:, 2 + s, :],
                                   ACT.Copy).then_inc(l.summed_out, 1)
                act.wait_ge(l.message_done, g + 3)
                act.wait_ge(l.retired, g + 1)
                act.activation(message[s][:, :, :].rearrange("p a d -> p (a d)"), ps_b[:, s, :],
                               ACT.Copy).then_inc(l.message_ready, 1)

            for l in layers:
                act.sem_inc(l.message_ready, 2)
            act.wait_ge(consts_ready, 2)
            for l in layers:
                with act.Fori(0, GROUPS // 2) as i:
                    step(l, 2 * i, 0, i)
                    step(l, 2 * i + 1, 1, i)

            act.wait_ge(stats_done, CHUNKS)
            act.activation(node_std[:, :, :], node_moments[:, :, :, 1], ACT.Sqrt, bias=eps_col[:, :]).then_inc(node_std_ready, 1)

            def relu_norm(c, s):
                p, j = shape_of(c)
                for r in range(j):
                    ins = act.activation(relu_ln[0:p, r, :], x1_in[s][0:p, r, :], ACT.Relu,
                                         scale=norm_now[s][0:p, 0, r:r + 1], bias=norm_now[s][0:p, 1, r:r + 1])
                return ins

            def gram(c, s, k):
                act.wait_ge(norm_picked, c + 1)
                act.wait_ge(gram_x_loaded[s], 16 * k + 16)
                act.wait_ge(gram_h, c + 2)
                relu_norm(c, s).then_inc(gram_relu, 1)
                act.wait_ge(gram_h, c + 3)
                act.wait_ge(gram_used, c + 1)
                p, j = shape_of(c)
                act.activation(gram_in[s][0:p, 0:j, 0, :], h[0:p, 0:j, :], ACT.Copy).then_inc(gram_hi, 1)
            chunk_schedule(act, gram)

            act.wait_ge(gram_used, CHUNKS + 2)
            act.activation(gram0[:, :], ps_a[:, 0, :], ACT.Copy)
            act.activation(gram1[:, :], ps_a[:, 1, 0:D + P], ACT.Copy).then_inc(bn_act, 1)

            act.wait_ge(bn_pe, 4)
            act.activation(bn_std[:, :], ps_b[:, 1, 0:MB], ACT.Sqrt, bias=eps_col[:, :]).then_inc(bn_act, 1)

            def prepare(n, s, k):
                act.wait_ge(norm_picked, CHUNKS + n + 1)
                act.wait_ge(main_loaded[s], 32 * k + 32)
                if not (isinstance(n, int) and n == 0):
                    act.wait_ge(h_ready, n)
                relu_norm(n, s).then_inc(ln_ready, 1)

            act.wait_ge(bn_ready, 1)
            prepare(0, 0, 0)

            def main(n, s, k):
                p, j = shape_of(n)
                w = p * j
                for kb in range(KB):
                    act.wait_ge(hT_done, KB * n + kb + 1)
                    act.activation(hT_hi[:, kb, 0:w], ps_a[:, kb, 0:w], ACT.Copy).then_inc(hT_hi_ready, 1)
                for m in range(MB):
                    act.wait_ge(up_done, MB * n + m + 1)
                    if m >= 2:
                        act.wait_ge(hid_lo_ready, MB * n + m - 1)
                    elif not (isinstance(n, int) and n == 0):
                        act.wait_ge(hid_lo_ready, MB * n + m - 1)
                    act.activation(hid[m % 2][:, 0:w], ps_a[:, 2 + m % 2, 0:w], ACT.Relu,
                                   scale=bn_scale[:, m:m + 1], bias=bn_bias[:, m:m + 1]).then_inc(hid_ready, 1)
                    if m >= 4 or not (isinstance(n, int) and n == 0):
                        act.wait_ge(down_done, MB * n + m - 3)
                    act.wait_ge(hid_ready, MB * n + m + 1)
                    act.activation(hid_hi[m % 4][:, 0:w], hid[m % 2][:, 0:w], ACT.Copy).then_inc(hid_hi_ready, 1)
                    if m == 4 and not (isinstance(n, int) and n == CHUNKS - 1):
                        prepare(n + 1, 1 - s, (k if s == 0 else k + 1))
            main_schedule(act, main)

        @block.vector
        def _(dve):
            class Chain:
                def __init__(self):
                    self.before, self.n = 0, 0

                def then(self, ins):
                    self.n += 1
                    ins.then_inc(dve_step, 1)

                def wait(self):
                    dve.wait_ge(dve_step, self.before + self.n)

            chain = Chain()

            def looped(count, per, body):
                start = chain.before + chain.n
                with dve.Fori(0, count) as i:
                    chain.before, chain.n = i * per + start, 0
                    body(i)
                    assert chain.n == per, chain.n
                chain.before, chain.n = start + count * per, 0

            dve.wait_ge(ids_loaded, 16 * 10)
            for n in range(2):
                view = lambda t: t[:, :].rearrange("p (g a) -> p g a", a=PAIR)
                chain.then(dve.tensor_copy(edge_info[n][:, :, 0:PAIR], view(target_ids[n])))
                chain.then(dve.tensor_copy(edge_info[n][:, :, PAIR:2 * PAIR], view(weights)))
                chain.then(dve.tensor_copy(edge_info[n][:, :, 2 * PAIR:3 * PAIR], view(dump_ids)))
                chain.wait()
                dve.tensor_tensor(edge_info[n][:, :, 2 * PAIR:3 * PAIR], edge_info[n][:, :, 2 * PAIR:3 * PAIR],
                                  edge_info[n][:, :, 0:PAIR], ALU.subtract).then_inc(info_built, 1)
            dve.wait_ge(info_built, 2)

            def pick_gather(l, g, s):
                dve.tensor_copy(gather_now[s][:, :], l.gather_ids[:, bass.ds(g * PAIR, PAIR)]).then_inc(l.gather_ready, 1)

            def edge_step(l, g, s, k, more):
                dve.tensor_copy(info_now[s][:, :], l.info[:, bass.ds(g, 1), :].rearrange("p g i -> p (g i)")).then_inc(l.info_ready, 1)
                dve.wait_ge(l.gathered[s], 16 * PAIR * (k + 1))
                for a in range(PAIR):
                    ins = dve.bn_stats(row_stats[:, a, :], gathered_rows[s][:, a, :])
                chain.then(ins)
                chain.wait()
                if more:
                    pick_gather(l, g + 2, s)
                else:
                    chain.then(dve.tensor_copy(shift[:, :], row_stats[:, :, 0]))
                for a in range(PAIR):
                    ins = dve.bn_aggr(row_moments[s][:, a, :], row_stats[:, a, :])
                ins.then_inc(l.moments_ready, 1)
                dve.wait_ge(l.targets_spread, g + 1)
                dve.wait_ge(l.info_ready, g + 1)
                for a in range(PAIR):
                    ins = dve.scalar_tensor_tensor(same_earlier[:, a, :], ps_b[:, 2 + s, 0:PAIR * P], info_now[s][:, a:a + 1],
                                                   earlier[:, a, :], ALU.is_equal, ALU.mult,
                                                   accum_out=n_earlier[:, a:a + 1])
                chain.then(ins)
                dve.wait_ge(l.std_ready, g + 1)
                chain.then(dve.reciprocal(row_norm[s][:, 0, :], row_std[s][:, :]))
                chain.wait()
                dve.scalar_tensor_tensor(row_norm[s][:, 1, :], row_moments[s][:, :, 0], -1.0, row_norm[s][:, 0, :],
                                         ALU.mult, ALU.mult).then_inc(l.norm_ready, 1)
                for a in range(PAIR):
                    if l.n == 0:
                        ins = dve.tensor_scalar(same[s][:, a, :], ps_b[:, 2 + s, 0:PAIR * P], info_now[s][:, a:a + 1],
                                                info_now[s][:, PAIR + a:PAIR + a + 1], ALU.is_equal, ALU.mult)
                    else:
                        ins = dve.tensor_scalar(same[s][:, a, :], ps_b[:, 2 + s, 0:PAIR * P], info_now[s][:, a:a + 1],
                                                None, ALU.is_equal)
                ins.then_inc(l.same_ready, 1)
                chain.wait()
                chain.then(dve.scalar_tensor_tensor(shift[:, :], n_earlier[:, :], 0.0, info_now[s][:, 2 * PAIR:3 * PAIR],
                                                    ALU.is_gt, ALU.mult))
                chain.wait()
                dve.wait_ge(l.retired, g + 1)
                dve.tensor_tensor(scatter_now[s][:, :], shift[:, :], info_now[s][:, 0:PAIR], ALU.add).then_inc(l.scatter_ready, 1)

            def node_step(c, s, k):
                p, j = shape_of(c)
                dve.wait_ge(stats_loaded[s], 16 * k + 16)
                for r in range(j):
                    ins = dve.bn_stats(node_stats[0:p, r, :], x1_in[s][0:p, r, :])
                chain.then(ins)
                chain.wait()
                dve.sem_inc(stats_taken, 1)
                for r in range(j):
                    ins = dve.bn_aggr(chunk_moments[0:p, r, :], node_stats[0:p, r, :])
                chain.then(ins)
                chain.wait()
                dve.tensor_copy(node_moments[0:p, bass.ds(c, 1), 0:j, :].rearrange("p c j t -> p (c j t)"),
                                chunk_moments[0:p, 0:j, :].rearrange("p j t -> p (j t)")).then_inc(stats_done, 1)

            dve.sem_inc(stats_taken, 2)
            dve.sem_inc(gram_h, 2)
            dve.sem_inc(gram_lo, 1)
            dve.wait_ge(consts_ready, 3)
            chain.then(dve.tensor_copy(ones_r[:, :], ones[:, :]))

            EDGE = 4
            for l in layers:
                for s in range(2):
                    if l.n == 1:
                        dve.wait_ge(layers[0].retired, GROUPS + 2)
                    pick_gather(l, s, s)
                if l.n == 1:
                    dve.wait_ge(w12_loaded, 16 * 6)
                    chain.then(dve.tensor_copy(w1_hi[:, :, :], w1_f[:, :, :]))
                    chain.then(dve.tensor_copy(w2_hl[:, :, 0, :], w2_f[:, :, :]))
                    chain.wait()
                    dve.tensor_tensor(w1_lo[:, :, :], w1_f[:, :, :], w1_hi[:, :, :].bitcast(F32), ALU.subtract)
                    dve.tensor_tensor(w2_hl[:, :, 1, :], w2_f[:, :, :], w2_hl[:, :, 0, :].bitcast(F32),
                                      ALU.subtract).then_inc(w12_split, 1)
                per = EDGE + (2 if l.n else 0)

                def body(i):
                    for s in range(2):
                        edge_step(l, 2 * i + s, s, i, True)
                        if l.n:
                            node_step(2 * i + s, s, i)
                looped(GROUPS // 2 - 1, 2 * per, body)
                for g in (GROUPS - 2, GROUPS - 1):
                    edge_step(l, g, g % 2, g // 2, False)
                    if l.n:
                        node_step(g, g % 2, g // 2)

            dve.wait_ge(node_std_ready, 1)
            chain.then(dve.reciprocal(node_rstd[:, :, :], node_std[:, :, :]))
            chain.wait()
            chain.then(dve.scalar_tensor_tensor(node_shift[:, :, :], node_moments[:, :, :, 0], -1.0, node_rstd[:, :, :],
                                                ALU.mult, ALU.mult))
            chain.wait()

            def pick_norm(c, s):
                dve.tensor_copy(norm_now[s][:, 0, :], node_rstd[:, bass.ds(c, 1), :].rearrange("p c j -> p (c j)"))
                dve.tensor_copy(norm_now[s][:, 1, :], node_shift[:, bass.ds(c, 1), :].rearrange("p c j -> p (c j)")).then_inc(norm_picked, 1)

            pick_norm(0, 0)
            pick_norm(1, 1)

            def gram(c, s, k):
                p, j = shape_of(c)
                dve.wait_ge(gram_relu, c + 1)
                dve.wait_ge(gram_a_loaded[s], 16 * k + 16)
                dve.wait_ge(gram_lo, c + 1)
                dve.wait_ge(gram_hi, c + 1)
                dve.tensor_tensor(h[0:p, 0:j, :], relu_ln[0:p, 0:j, :], agg_in[s][0:p, 0:j, :], ALU.add).then_inc(gram_h, 1)
                if not isinstance(c, int):
                    pick_norm(c + 2, s)
                elif c + 2 < CHUNKS:
                    pick_norm(c + 2, s)
                dve.wait_ge(gram_hi, c + 2)
                dve.tensor_tensor(gram_in[s][0:p, 0:j, 1, :], h[0:p, 0:j, :], gram_in[s][0:p, 0:j, 0, :].bitcast(F32),
                                  ALU.subtract).then_inc(gram_lo, 1)
            chunk_schedule(dve, gram)
            pick_norm(0, 0)
            pick_norm(1, 1)

            dve.wait_ge(gram_used, CHUNKS + 2)
            chain.then(dve.tensor_scalar(gram_sum[:, :], ps_a[:, 2, 0:D], 1.0 / N, None, ALU.mult))
            chain.wait()
            dve.scalar_tensor_tensor(mu_row[:, :], ps_a[:, 2, D:2 * D], 1.0 / N, gram_sum[:, :], ALU.mult,
                                     ALU.add).then_inc(bn_act, 1)
            dve.wait_ge(bn_act, 2)
            chain.then(dve.tensor_tensor(cov[0][:, :], gram0[:, 0:D], gram0[:, D:2 * D], ALU.add))
            chain.then(dve.tensor_tensor(cov[1][:, P:D], gram1[:, 0:P], gram1[:, D:D + P], ALU.add))
            dve.wait_ge(bn_pe, 1)
            chain.wait()
            chain.then(dve.tensor_tensor(cov[0][:, :], cov[0][:, :], ps_b[:, 0, 0:D], ALU.add))
            chain.then(dve.tensor_tensor(cov[1][:, P:D], cov[1][:, P:D], ps_b[:, 0, D:D + P], ALU.add))
            chain.then(dve.tensor_scalar(mu_col[:, :], ps_b[:, 3, 0:KB], 1.0 / P, None, ALU.mult))
            chain.wait()
            chain.then(dve.scalar_tensor_tensor(cov[0][:, :], cov[0][:, :], 1.0 / N, ps_b[:, 1, 0:D], ALU.mult, ALU.subtract))
            dve.scalar_tensor_tensor(cov[1][:, P:D], cov[1][:, P:D], 1.0 / N, ps_b[:, 2, P:D], ALU.mult,
                                     ALU.subtract).then_inc(bn_act, 1)
            dve.wait_ge(bn_pe, 2)
            dve.tensor_copy(cov[1][:, 0:P], ps_b[:, 0, 0:P]).then_inc(bn_act, 1)
            dve.wait_ge(bn_pe, 3)
            for i in range(KB):
                ins = dve.tensor_tensor(w1_cov[:, i, :].rearrange("p (a n) -> p a n", a=2),
                                        w1_f[:, i, :].rearrange("p (a n) -> p a n", a=2),
                                        ps_a[:, 2 * i:2 * i + 2, :], ALU.mult)
            ins.then_inc(bn_act, 1)
            dve.wait_ge(bn_pe, 4)
            chain.then(dve.tensor_tensor(bn_mean[:, :], ps_b[:, 2, 0:MB], b1_v, ALU.add))
            dve.wait_ge(bn_act, 6)
            chain.then(dve.reciprocal(bn_scale[:, :], bn_std[:, :]))
            chain.wait()
            chain.then(dve.tensor_tensor(bn_scale[:, :], bn_scale[:, :], gamma_v, ALU.mult))
            chain.then(dve.tensor_tensor(bn_mean[:, :], b1_v, bn_mean[:, :], ALU.subtract))
            chain.wait()
            chain.then(dve.tensor_tensor(bn_bias[:, :], bn_scale[:, :], bn_mean[:, :], ALU.mult))
            chain.wait()
            dve.tensor_tensor(bn_bias[:, :], bn_bias[:, :], beta_v, ALU.add).then_inc(bn_ready, 1)

            def add_agg(n, s, k):
                p, j = shape_of(n)
                dve.wait_ge(ln_ready, n + 1)
                dve.wait_ge(main_loaded[s], 32 * k + 32)
                dve.tensor_tensor(h[0:p, 0:j, :], relu_ln[0:p, 0:j, :], agg_in[s][0:p, 0:j, :], ALU.add).then_inc(h_ready, 1)

            def read_down(n, s, k):
                p, j = shape_of(n)
                dve.wait_ge(down_done, MB * n + MB)
                dve.wait_ge(out_retired, n + 1)
                chain.then(dve.tensor_tensor(out_sb[s][0:p, 0:j, :], ps_b[0:p, 0:j, 0:D],
                                             b2_bc[0:p, :].rearrange("p (a d) -> p a d", a=1).to_broadcast([p, j, D]), ALU.add))
                chain.wait()
                dve.tensor_tensor(out_sb[s][0:p, 0:j, :], out_sb[s][0:p, 0:j, :], ps_b[0:p, 0:j, D:2 * D],
                                  ALU.add).then_inc(down_read, 1)

            def finish(n, s):
                p, j = shape_of(n)
                dve.wait_ge(down_read, n + 1)
                dve.scalar_tensor_tensor(out_sb[s][0:p, 0:j, :], out_sb[s][0:p, 0:j, :], 0.0, x1_in[s][0:p, 0:j, :],
                                         ALU.max, ALU.add).then_inc(out_ready, 1)

            add_agg(0, 0, 0)

            def main(n, s, k):
                p, j = shape_of(n)
                w = p * j
                first = isinstance(n, int) and n == 0
                for kb in range(KB):
                    dve.wait_ge(hT_hi_ready, KB * n + kb + 1)
                    dve.tensor_tensor(hT_lo[:, kb, 0:w], ps_a[:, kb, 0:w], hT_hi[:, kb, 0:w].bitcast(F32),
                                      ALU.subtract).then_inc(hT_lo_ready, 1)
                if not first:
                    read_down(n - 1, 1 - s, k)
                for m in range(MB):
                    dve.wait_ge(hid_hi_ready, MB * n + m + 1)
                    if m >= 4 or not first:
                        dve.wait_ge(down_done, MB * n + m - 3)
                    dve.tensor_tensor(hid_lo[m % 4][:, 0:w], hid[m % 2][:, 0:w], hid_hi[m % 4][:, 0:w].bitcast(F32),
                                      ALU.subtract).then_inc(hid_lo_ready, 1)
                    if m == 1 and not first:
                        finish(n - 1, 1 - s)
                    if m == 6 and not (isinstance(n, int) and n == CHUNKS - 1):
                        add_agg(n + 1, 1 - s, (k if s == 0 else k + 1))
                    if m == 2 and not (isinstance(n, int) and n + 2 >= CHUNKS):
                        pick_norm(n + 2, s)
            main(0, 0, 0)
            def pair(i):
                main(2 * i + 1, 1, i)
                main(2 * i + 2, 0, i + 1)
            looped(MAIN_PAIRS, 2, pair)
            for n in range(CHUNKS - 3, CHUNKS):
                main(n, n % 2, n // 2)
            read_down(CHUNKS - 1, (CHUNKS - 1) % 2, (CHUNKS - 1) // 2)
            finish(CHUNKS - 1, (CHUNKS - 1) % 2)

        @block.tensor
        def _(pe):
            for l in layers:
                pe.sem_inc(l.message_done, 2)
            pe.sem_inc(layers[0].summed, 2)
            pe.sem_inc(gram_used, 2)
            pe.sem_inc(gram_hi, 1)
            pe.wait_ge(consts_ready, 3)
            pe.wait_ge(w_loaded, 16)
            for k in range(KB):
                for o in range(KB):
                    ins = pe.transpose(ps_a[:, 0, k * D + o * P:k * D + (o + 1) * P], w_rows[:, o, k * P:(k + 1) * P], ident[:, :])
            ins.then_inc(wT_done, 1)
            pe.wait_ge(wT_ready, 1)

            def step(l, g, s, k):
                pe.wait_ge(l.info_ready, g + 1)
                for b in range(PAIR):
                    ins = pe.matmul(ps_b[:, 2 + s, b * P:(b + 1) * P], info_now[s][:, b:b + 1].to_broadcast([P, P]),
                                    ident[:, :], start=True, stop=True)
                ins.then_inc(l.targets_spread, 1)
                pe.wait_ge(l.same_ready, g + 1)
                pe.wait_ge(l.normed_ready, g + 1)
                if l.n == 0:
                    for kb in range(KB):
                        for a in range(PAIR):
                            ins = pe.matmul(ps_a[:, 2 + s, kb * PAIR * P:(kb + 1) * PAIR * P],
                                            normed[s][:, a, kb * P:(kb + 1) * P], same[s][:, a, :],
                                            start=(a == 0), stop=(a == PAIR - 1))
                    ins.then_inc(l.summed, 1)
                    pe.wait_ge(l.summed_out, g + 1)
                    pe.wait_ge(l.message_ready, g + 1)
                    for b in range(PAIR):
                        for kb in range(KB):
                            ins = pe.matmul(ps_b[:, s, b * D:(b + 1) * D], summedT[s][:, kb, b * P:(b + 1) * P],
                                            wT[:, kb, :], start=(kb == 0), stop=(kb == KB - 1))
                else:
                    pe.wait_ge(l.message_ready, g + 1)
                    for b in range(PAIR):
                        for a in range(PAIR):
                            ins = pe.matmul(ps_b[:, s, b * D:(b + 1) * D], same[s][:, a, b * P:(b + 1) * P],
                                            normed[s][:, a, :], start=(a == 0), stop=(a == PAIR - 1))
                ins.then_inc(l.message_done, 1)

            for l in layers:
                with pe.Fori(0, GROUPS // 2) as i:
                    step(l, 2 * i, 0, i)
                    step(l, 2 * i + 1, 1, i)

            def gram(c, s, k):
                p, j = shape_of(c)
                pe.wait_ge(gram_lo, c + 2)
                for r in range(j):
                    first = isinstance(c, int) and c == 0 and r == 0
                    last = isinstance(c, int) and c == CHUNKS - 1 and r == j - 1
                    both = gram_in[s][0:p, r, :, :].rearrange("p t d -> p (t d)")
                    pe.matmul(ps_a[:, 0, :], both[:, 0:P], both, start=first, stop=last)
                    pe.matmul(ps_a[:, 1, 0:D + P], both[:, P:D], both[:, P:2 * D], start=first, stop=last)
                    ins = pe.matmul(ps_a[:, 2, :], ones_r[0:p, :], both, start=first, stop=last)
                ins.then_inc(gram_used, 1)
            gram(0, 0, 0)
            gram(1, 1, 0)
            with pe.Fori(0, FULL_CHUNKS // 2 - 1) as i:
                gram(2 * i + 2, 0, i + 1)
                gram(2 * i + 3, 1, i + 1)
            for c in range(FULL_CHUNKS // 2 * 2, CHUNKS):
                gram(c, c % 2, c // 2)

            pe.wait_ge(bn_act, 2)
            pe.transpose(ps_b[:, 0, 0:P], gram0[:, D:D + P], ident[:, :])
            pe.transpose(ps_b[:, 0, P:D], gram1[:, P:D], ident[:, :])
            pe.transpose(ps_b[:, 0, D:D + P], gram1[:, D:D + P], ident[:, :])
            for k in range(KB):
                pe.matmul(ps_b[:, 1 + k, 0:D], mu_row[0:1, k * P:(k + 1) * P], mu_row[0:1, :], start=True, stop=True)
            for k in range(KB):
                ins = pe.matmul(ps_b[:, 3, k:k + 1], mu_row[:, k * P:(k + 1) * P], ones[:, 0:1], start=True, stop=True)
            ins.then_inc(bn_pe, 1)
            pe.wait_ge(bn_act, 3)
            pe.transpose(ps_b[:, 0, 0:P], cov[0][:, P:D], ident[:, :]).then_inc(bn_pe, 1)
            pe.wait_ge(bn_act, 4)
            for i in range(KB):
                for a in range(2):
                    for k in range(KB):
                        ins = pe.matmul(ps_a[:, 2 * i + a, :], cov[k][:, i * P:(i + 1) * P], w1_f[:, k, a * 512:(a + 1) * 512],
                                        start=(k == 0), stop=(k == KB - 1))
            ins.then_inc(bn_pe, 1)
            pe.wait_ge(bn_act, 5)
            for m in range(MB):
                for i in range(KB):
                    pe.matmul(ps_b[:, 1, m:m + 1], w1_cov[:, i, m * P:(m + 1) * P], ones[:, 0:1],
                              start=(i == 0), stop=(i == KB - 1))
                for k in range(KB):
                    ins = pe.matmul(ps_b[:, 2, m:m + 1], w1_f[:, k, m * P:(m + 1) * P], mu_col[:, k:k + 1],
                                    start=(k == 0), stop=(k == KB - 1))
            ins.then_inc(bn_pe, 1)
            pe.wait_ge(bn_ready, 1)
            pe.wait_ge(w12_split, 1)

            def transpose_h(n):
                p, j = shape_of(n)
                pe.wait_ge(h_ready, n + 1)
                for kb in range(KB):
                    for r in range(j):
                        ins = pe.transpose(ps_a[:, kb, r * p:(r + 1) * p], h[0:p, r, kb * P:(kb + 1) * P], ident[0:p, 0:p])
                    ins.then_inc(hT_done, 1)

            def up(n, m):
                p, j = shape_of(n)
                w = p * j
                if m == 0:
                    pe.wait_ge(hT_hi_ready, KB * n + KB)
                    pe.wait_ge(hT_lo_ready, KB * n + KB)
                if m >= 2 or not (isinstance(n, int) and n == 0):
                    pe.wait_ge(hid_ready, MB * n + m - 1)
                cols = slice(m * P, (m + 1) * P)
                terms = [(w_part, h_part, kb) for kb in range(KB)
                         for w_part, h_part in ((w1_hi, hT_hi), (w1_hi, hT_lo), (w1_lo, hT_hi))]
                for t, (w_part, h_part, kb) in enumerate(terms):
                    ins = pe.matmul(ps_a[:, 2 + m % 2, 0:w], w_part[:, kb, cols], h_part[:, kb, 0:w],
                                    start=(t == 0), stop=(t == len(terms) - 1))
                ins.then_inc(up_done, 1)

            def down(n, m):
                p, j = shape_of(n)
                pe.wait_ge(hid_hi_ready, MB * n + m + 1)
                pe.wait_ge(hid_lo_ready, MB * n + m + 1)
                if m == 0 and not (isinstance(n, int) and n == 0):
                    pe.wait_ge(down_read, n)
                w2 = w2_hl[:, m, :, :].rearrange("p t d -> p (t d)")
                for r in range(j):
                    cols = slice(r * p, (r + 1) * p)
                    pe.matmul(ps_b[0:p, r, :], hid_hi[m % 4][:, cols], w2, start=(m == 0), stop=(m == MB - 1), skip_group_check=True)
                    ins = pe.matmul(ps_b[0:p, r, 0:D], hid_lo[m % 4][:, cols], w2[:, 0:D], start=False, stop=(m == MB - 1), skip_group_check=True)
                ins.then_inc(down_done, 1)

            def main(n, s, k):
                transpose_h(n)
                if not (isinstance(n, int) and n == 0):
                    down(n - 1, MB - 2)
                    down(n - 1, MB - 1)
                up(n, 0)
                up(n, 1)
                for m in range(2, MB):
                    up(n, m)
                    down(n, m - 2)
            main_schedule(pe, main)
            down(CHUNKS - 1, MB - 2)
            down(CHUNKS - 1, MB - 1)


def kernel(x, src, dst, edge_weight, L0_gnn_W, L1_gnn_W1, L1_gnn_b1, L1_gnn_gamma, L1_gnn_beta, L1_gnn_W2, L1_gnn_b2):
    import numpy as np
    import concourse.bacc as bacc
    from concourse import mybir
    from concourse.bass_utils import run_bass_kernel_spmd

    nc = bacc.Bacc("TRN2", target_bir_lowering=False, num_devices=1)
    given = dict(x=x, src=src, dst=dst, edge_weight=edge_weight, W=L0_gnn_W, W1=L1_gnn_W1, b1=L1_gnn_b1,
                 gamma=L1_gnn_gamma, beta=L1_gnn_beta, W2=L1_gnn_W2, b2=L1_gnn_b2)
    arrays = {f"in_{name}": np.ascontiguousarray(a) for name, a in given.items()}
    aps = {name: nc.dram_tensor(f"in_{name}", arrays[f"in_{name}"].shape,
                                mybir.dt.from_np(arrays[f"in_{name}"].dtype), kind="ExternalInput").ap()
           for name in given}
    out = nc.dram_tensor("out", arrays["in_x"].shape, mybir.dt.float32, kind="ExternalOutput").ap()
    gnn_program(nc, out=out, **aps)
    result = run_bass_kernel_spmd(nc, [arrays], core_ids=[0])
    return result.results[0]["out"]
```

```python
def gnn_program(nc, x, src, dst, edge_weight, W, W1, b1, gamma, beta, W2, b2, out):
    from contextlib import ExitStack

    import concourse.bass as bass
    from concourse import mybir

    F32, F32R, I32 = mybir.dt.float32, mybir.dt.float32r, mybir.dt.int32
    ALU = mybir.AluOpType
    ACT = mybir.ActivationFunctionType

    P = 128
    N, D = x.shape
    E = src.shape[0]
    HID = W1.shape[1]
    KB = D // P
    MB = HID // P
    EPS = 1e-5

    PAIR = 2
    COLS = -(-E // (P * PAIR)) * PAIR
    GROUPS = COLS // PAIR
    FULL_EDGE_ROWS = E // COLS
    LAST_EDGES = E - FULL_EDGE_ROWS * COLS
    assert GROUPS % 2 == 0 and FULL_EDGE_ROWS == P - 1
    DUMP_ROWS = P * PAIR
    AHEAD = 4

    ROWS = 4
    CHUNK = P * ROWS
    FULL_CHUNKS = N // CHUNK
    TAIL_NODES = N - FULL_CHUNKS * CHUNK
    TAIL_ROWS = 3
    TAIL_P = TAIL_NODES // TAIL_ROWS
    assert TAIL_P * TAIL_ROWS == TAIL_NODES and TAIL_P <= P and TAIL_P % 16 == 0
    CHUNKS = FULL_CHUNKS + 1
    assert CHUNKS == GROUPS

    ZERO_PIECES = 50
    ZERO_P = 80
    ZERO_LEN = N * D // ZERO_PIECES // ZERO_P
    assert ZERO_PIECES * ZERO_P * ZERO_LEN == N * D and ZERO_LEN >= DUMP_ROWS * D // P
    COPY_PIECES = 4
    COPY_ROWS = 500
    assert N % (COPY_PIECES * COPY_ROWS) == 0

    x1_table = nc.dram_tensor("x1_table", (N + DUMP_ROWS, D), F32, kind="Internal").ap()
    agg_table = nc.dram_tensor("agg_table", (N + DUMP_ROWS, D), F32, kind="Internal").ap()

    def full_chunks(table):
        return table[0:FULL_CHUNKS * CHUNK, :].rearrange("(c p j) d -> c p (j d)", p=P, j=ROWS)

    def tail_chunk(table):
        return table[FULL_CHUNKS * CHUNK:N, :].rearrange("(p j) d -> p (j d)", j=TAIL_ROWS)

    with ExitStack() as ctx:
        def sb(name, shape, dt=F32):
            return ctx.enter_context(nc.sbuf_tensor(name, shape, dt))

        def sem(name):
            return ctx.enter_context(nc.semaphore(name))

        ident = sb("ident", [P, P])
        ones = sb("ones", [P, P])
        ones_r = sb("ones_r", [P, P], F32R)
        zeros = sb("zeros", [P, ZERO_LEN])
        earlier = sb("earlier", [P, PAIR, PAIR * P])
        gather_ids = [sb(f"gather_ids{i}", [P, COLS], I32) for i in range(2)]
        target_ids = [sb(f"target_ids{i}", [P, COLS], I32) for i in range(2)]
        dump_ids = sb("dump_ids", [P, COLS], I32)
        weights = sb("weights", [P, COLS])
        edge_info = [sb(f"edge_info{i}", [P, GROUPS, 3 * PAIR]) for i in range(2)]
        info_now = [sb(f"info_now{s}", [P, 3 * PAIR]) for s in range(AHEAD)]
        gather_now = [sb(f"gather_now{s}", [P, PAIR], I32) for s in range(AHEAD)]
        scatter_now = [sb(f"scatter_now{s}", [P, PAIR], I32) for s in range(AHEAD)]
        gathered_rows = [sb(f"gathered_rows{s}", [P, PAIR, D]) for s in range(AHEAD)]
        row_norm = [sb(f"row_norm{s}", [P, 2, PAIR]) for s in range(2)]
        row_stats = sb("row_stats", [P, PAIR, 6])
        row_moments = [sb(f"row_moments{s}", [P, PAIR, 2]) for s in range(2)]
        row_std = [sb(f"row_std{s}", [P, PAIR]) for s in range(2)]
        eps_col = sb("eps_col", [P, 1])
        normed = [sb(f"normed{s}", [P, PAIR, D]) for s in range(2)]
        same = [sb(f"same{s}", [P, PAIR, PAIR * P]) for s in range(2)]
        same_earlier = sb("same_earlier", [P, PAIR, PAIR * P])
        n_earlier = sb("n_earlier", [P, PAIR])
        shift = sb("shift", [P, PAIR])
        summedT = [sb(f"summedT{s}", [P, KB, PAIR * P]) for s in range(2)]
        message = [sb(f"message{s}", [P, PAIR, D]) for s in range(2)]
        x1_in = [sb(f"x1_in{s}", [P, ROWS, D]) for s in range(2)]
        agg_in = [sb(f"agg_in{s}", [P, ROWS, D]) for s in range(2)]
        node_stats = sb("node_stats", [P, ROWS, 6])
        chunk_moments = sb("chunk_moments", [P, ROWS, 2])
        node_moments = sb("node_moments", [P, CHUNKS, ROWS, 2])
        node_rstd = sb("node_rstd", [P, CHUNKS, ROWS])
        node_std = sb("node_std", [P, CHUNKS, ROWS])
        node_shift = sb("node_shift", [P, CHUNKS, ROWS])
        norm_now = [sb(f"norm_now{s}", [P, 2, ROWS]) for s in range(2)]
        relu_ln = [sb(f"relu_ln{s}", [P, ROWS, D]) for s in range(2)]
        h = [sb(f"h{s}", [P, ROWS, D]) for s in range(2)]
        gram_in = [sb(f"gram_in{s}", [P, ROWS, 2, D], F32R) for s in range(2)]
        w_rows = sb("w_rows", [P, KB, D])
        wT = sb("wT", [P, KB, D])
        w1_f = sb("w1_f", [P, KB, HID])
        w1_hi = sb("w1_hi", [P, KB, HID], F32R)
        w1_lo = sb("w1_lo", [P, KB, HID], F32R)
        w2_f = sb("w2_f", [P, MB, D])
        w2_hl = sb("w2_hl", [P, MB, 2, D], F32R)
        b2_bc = sb("b2_bc", [P, D])
        hid_vec = sb("hid_vec", [P, 3, MB])
        b1_v, gamma_v, beta_v = (hid_vec[:, i, :] for i in range(3))
        gram0 = sb("gram0", [P, 2 * D])
        gram_sum = sb("gram_sum", [P, D])
        gram1 = sb("gram1", [P, D + P])
        mu_row = sb("mu_row", [P, D])
        mu_col = sb("mu_col", [P, KB])
        cov = [sb(f"cov{k}", [P, D]) for k in range(KB)]
        w1_cov = w2_f[:, :, :].rearrange("p m d -> p (m d)").rearrange("p (k n) -> p k n", k=KB)
        bn_scale = sb("bn_scale", [P, MB])
        bn_std = sb("bn_std", [P, MB])
        bn_bias = sb("bn_bias", [P, MB])
        bn_mean = sb("bn_mean", [P, MB])
        hT_hi = sb("hT_hi", [P, KB, CHUNK], F32R)
        hT_lo = sb("hT_lo", [P, KB, CHUNK], F32R)
        hid = [sb(f"hid{i}", [P, CHUNK]) for i in range(2)]
        hid_hi = [sb(f"hid_hi{i}", [P, CHUNK], F32R) for i in range(4)]
        hid_lo = [sb(f"hid_lo{i}", [P, CHUNK], F32R) for i in range(4)]
        out_sb = [zeros[:, s * ROWS * D:(s + 1) * ROWS * D].rearrange("p (j d) -> p j d", j=ROWS) for s in range(2)]

        ps_a = ctx.enter_context(nc.psum_tensor("ps_a", [P, 4, 512], F32))
        ps_b = ctx.enter_context(nc.psum_tensor("ps_b", [P, 4, 512], F32))

        ids_blank = sem("ids_blank")
        consts_ready = sem("consts_ready")
        ids_loaded = sem("ids_loaded")
        w_loaded = sem("w_loaded")
        w12_loaded = sem("w12_loaded")
        x1_copied = sem("x1_copied")
        dump_zeroed = sem("dump_zeroed")
        agg_zeroed = sem("agg_zeroed")
        info_built = sem("info_built")
        wT_done = sem("wT_done")
        wT_ready = sem("wT_ready")
        dve_step = sem("dve_step")
        pool_gate = sem("pool_gate")

        class Layer:
            def __init__(self, n):
                self.n = n
                self.gather_from = (x, x1_table)[n]
                self.scatter_to = (x1_table, agg_table)[n]
                self.gather_ids = gather_ids[1 - n]
                self.info = edge_info[n]
                self.info_ready = sem(f"info_ready_L{n}")
                self.gather_ready = sem(f"gather_ready_L{n}")
                self.gathered = [sem(f"gathered_L{n}_{s}") for s in range(AHEAD)]
                self.moments_ready = sem(f"moments_ready_L{n}")
                self.std_ready = sem(f"std_ready_L{n}")
                self.norm_ready = sem(f"norm_ready_L{n}")
                self.normed_ready = sem(f"normed_ready_L{n}")
                self.targets_spread = sem(f"targets_spread_L{n}")
                self.same_ready = sem(f"same_ready_L{n}")
                self.scatter_ready = sem(f"scatter_ready_L{n}")
                self.summed = sem(f"summed_L{n}")
                self.summed_out = sem(f"summed_out_L{n}")
                self.message_done = sem(f"message_done_L{n}")
                self.message_ready = sem(f"message_ready_L{n}")
                self.scattered = [sem(f"scattered_L{n}_{s}") for s in range(2)]
                self.retired = sem(f"retired_L{n}")

        layers = [Layer(0), Layer(1)]

        stats_loaded = [sem(f"stats_loaded{s}") for s in range(2)]
        stats_taken = sem("stats_taken")
        stats_done = sem("stats_done")
        node_std_ready = sem("node_std_ready")
        gram_x_loaded = [sem(f"gram_x_loaded{s}") for s in range(2)]
        gram_a_loaded = [sem(f"gram_a_loaded{s}") for s in range(2)]
        norm_picked = sem("norm_picked")
        gram_relu = sem("gram_relu")
        gram_h = sem("gram_h")
        gram_hi = sem("gram_hi")
        gram_lo = sem("gram_lo")
        gram_used = sem("gram_used")
        bn_pe = sem("bn_pe")
        bn_act = sem("bn_act")
        bn_ready = sem("bn_ready")
        w12_split = sem("w12_split")

        main_loaded = [sem(f"main_loaded{s}") for s in range(2)]
        ln_ready = sem("ln_ready")
        h_ready = sem("h_ready")
        hT_done = sem("hT_done")
        hT_hi_ready = sem("hT_hi_ready")
        hT_lo_ready = sem("hT_lo_ready")
        up_done = sem("up_done")
        hid_ready = sem("hid_ready")
        hid_hi_ready = sem("hid_hi_ready")
        hid_lo_ready = sem("hid_lo_ready")
        down_done = sem("down_done")
        down_read = sem("down_read")
        out_ready = sem("out_ready")
        out_stored = [sem(f"out_stored{s}") for s in range(2)]
        out_retired = sem("out_retired")

        block = ctx.enter_context(nc.Block())

        class Turn:
            def __init__(self, i, per, base):
                self.i, self.per, self.base = i, per, base

            def __add__(self, d):
                return Turn(self.i, self.per, self.base + d)

            @property
            def n(self):
                return self.i * self.per + self.base if self.per else self.base

            def slot(self, slots):
                assert self.per % slots == 0
                return self.base % slots

            def use(self, slots):
                return self.i * (self.per // slots) + self.base // slots if self.per else self.base // slots

            def below(self, end):
                return self.per > 0 or 0 <= self.base < end

        def turns(eng, total, head, tail, step, loop=None):
            for t in range(head):
                step(Turn(0, 0, t))
            passes = (total - head - tail) // AHEAD

            def body(i):
                for u in range(AHEAD):
                    step(Turn(i, AHEAD, head + u))
            if loop:
                loop(passes, body)
            else:
                with eng.Fori(0, passes) as i:
                    body(i)
            for t in range(head + passes * AHEAD, total):
                step(Turn(0, 0, t))

        MAIN_PAIRS = (CHUNKS - 4) // 2
        assert CHUNKS == 4 + 2 * MAIN_PAIRS

        def shape_of(n):
            return (TAIL_P, TAIL_ROWS) if isinstance(n, int) and n == CHUNKS - 1 else (P, ROWS)

        def main_schedule(eng, step):
            step(0, 0, 0)
            with eng.Fori(0, MAIN_PAIRS) as i:
                step(2 * i + 1, 1, i)
                step(2 * i + 2, 0, i + 1)
            for n in range(CHUNKS - 3, CHUNKS):
                step(n, n % 2, n // 2)

        def chunk_schedule(eng, step, single=2):
            with eng.Fori(0, (CHUNKS - single) // 2) as i:
                step(2 * i, 0, i)
                step(2 * i + 1, 1, i)
            for c in range(CHUNKS - single, CHUNKS):
                step(c, c % 2, c // 2)

        def chunk_of(table, c):
            if isinstance(c, int) and c == CHUNKS - 1:
                return tail_chunk(table)
            return full_chunks(table)[bass.ds(c, 1), :, :].rearrange("c p e -> p (c e)")

        def tile_of(tile, c):
            p, j = shape_of(c)
            return tile[0:p, 0:j, :].rearrange("p j d -> p (j d)")

        @block.sync
        def _(sp):
            sp.sem_inc(out_retired, 2)
            sp.wait_ge(ids_blank, 1)
            def load_edges(tile, ids):
                sp.dma_start(tile[0:FULL_EDGE_ROWS, :],
                             ids[0:FULL_EDGE_ROWS * COLS].rearrange("(p c) -> p c", c=COLS)).then_inc(ids_loaded, 16)
                sp.dma_start(tile[FULL_EDGE_ROWS:P, 0:LAST_EDGES],
                             ids[FULL_EDGE_ROWS * COLS:E].rearrange("(p c) -> p c", p=1)).then_inc(ids_loaded, 16)
            for i, ids in ((1, dst), (0, src)):
                load_edges(gather_ids[i], ids)
                load_edges(target_ids[i], ids)
            load_edges(weights, edge_weight)
            sp.dma_start(w_rows[:, :, :], W.rearrange("(b p) i -> p b i", p=P)).then_inc(w_loaded, 16)
            for i in range(COPY_PIECES):
                rows = N // COPY_PIECES
                a = x[i * rows:(i + 1) * rows, :].rearrange("(a b) d -> a (b d)", b=rows // COPY_ROWS)
                b = x1_table[i * rows:(i + 1) * rows, :].rearrange("(a b) d -> a (b d)", b=rows // COPY_ROWS)
                sp.dma_start(b, a).then_inc(x1_copied, 16)
            sp.dma_start(w1_f[:, :, :], W1.rearrange("(k p) n -> p k n", p=P)).then_inc(w12_loaded, 16)
            sp.dma_start(w2_f[:, :, :], W2.rearrange("(m p) n -> p m n", p=P)).then_inc(w12_loaded, 16)
            sp.dma_start(b2_bc[:, :], b2.rearrange("(a n) -> a n", a=1).to_broadcast([P, D])).then_inc(w12_loaded, 16)
            with nc.allow_non_contiguous_dma(reason="three vectors of HID values, once"):
                for i, v in enumerate((b1, gamma, beta)):
                    sp.dma_start(hid_vec[:, i, :], v.rearrange("(m p) -> p m", p=P)).then_inc(w12_loaded, 16)
            sp.wait_ge(consts_ready, 1)
            for table in (x1_table, agg_table):
                sp.dma_start(table[N:N + DUMP_ROWS, :].rearrange("(p j) d -> p (j d)", p=P),
                             zeros[:, 0:PAIR * D]).then_inc(dump_zeroed, 16)
            agg_pieces = agg_table[0:N, :].rearrange("n d -> (n d)").rearrange("(i p e) -> i p e", i=ZERO_PIECES, p=ZERO_P)
            with sp.Fori(0, ZERO_PIECES) as i:
                sp.wait_ge(layers[0].normed_ready, i + 1)
                sp.dma_start(agg_pieces[bass.ds(i, 1), :, :].rearrange("i p e -> p (i e)"),
                             zeros[0:ZERO_P, :]).then_inc(agg_zeroed, 16)

            sp.wait_ge(layers[0].retired, GROUPS + AHEAD)

            def load_stats(c, s, k):
                sp.wait_ge(stats_taken, c + 1)
                sp.dma_start(tile_of(x1_in[s], c), chunk_of(x1_table, c)).then_inc(stats_loaded[s], 16)
            chunk_schedule(sp, load_stats)

            sp.wait_ge(stats_taken, CHUNKS + 2)
            sp.wait_ge(layers[1].retired, GROUPS + AHEAD)

            def load_gram(c, s, k):
                sp.wait_ge(gram_h, c + 1)
                sp.dma_start(tile_of(x1_in[s], c), chunk_of(x1_table, c)).then_inc(gram_x_loaded[s], 16)
                sp.dma_start(tile_of(agg_in[s], c), chunk_of(agg_table, c)).then_inc(gram_a_loaded[s], 16)
            chunk_schedule(sp, load_gram)
            sp.wait_ge(gram_h, CHUNKS + 2)

            def load_main(n, s):
                sp.dma_start(tile_of(x1_in[s], n), chunk_of(x1_table, n)).then_inc(main_loaded[s], 16)
                sp.dma_start(tile_of(agg_in[s], n), chunk_of(agg_table, n)).then_inc(main_loaded[s], 16)

            def store(n, s):
                sp.dma_start(chunk_of(out, n), tile_of(out_sb[s], n)).then_inc(out_stored[s], 16)

            load_main(0, 0)
            load_main(1, 1)
            def load_and_store(n, s, k):
                sp.wait_ge(out_ready, n + 1)
                load_main(n + 2, s)
                store(n, s)
                sp.wait_ge(out_stored[s], 16 * k + 16)
                sp.sem_inc(out_retired, 1)
            with sp.Fori(0, (CHUNKS - 4) // 2) as i:
                load_and_store(2 * i, 0, i)
                load_and_store(2 * i + 1, 1, i)
            load_and_store(CHUNKS - 4, 0, (CHUNKS - 4) // 2)
            load_and_store(CHUNKS - 3, 1, (CHUNKS - 4) // 2)
            for n in (CHUNKS - 2, CHUNKS - 1):
                sp.wait_ge(out_ready, n + 1)
                store(n, n % 2)
            for s in range(2):
                sp.wait_ge(out_stored[s], 16 * (CHUNKS // 2))

        @block.gpsimd
        def _(pool):
            dump_pattern = [[0, GROUPS], [1, PAIR]]
            for t in (dump_ids, target_ids[0], target_ids[1]):
                pool.iota(t[:, :], pattern=dump_pattern, base=N, channel_multiplier=PAIR)
            pool.memset(gather_ids[0][:, :], 0)
            pool.memset(gather_ids[1][:, :], 0)
            pool.memset(weights[:, :], 0.0).then_inc(ids_blank, 1)
            pool.memset(zeros[:, :], 0.0).then_inc(consts_ready, 1)
            pool.memset(node_moments[:, :, :, :], 1.0)
            pool.memset(eps_col[:, :], EPS)
            pool.memset(ident[:, :], 0.0)
            pool.memset(earlier[:, :, :], 0.0)
            pool.memset(ones[:, :], 1.0).then_inc(consts_ready, 1)
            pool.wait_ge(consts_ready, 2)
            pool.affine_select(out=ident[:, :], in_=ident[:, :], compare_op=ALU.not_equal, fill=1.0,
                               base=0, pattern=[[-1, P]], channel_multiplier=1)
            pool.tensor_copy(earlier[:, 1, 0:P], ones[:, :])
            pool.affine_select(out=earlier[:, 0, 0:P], in_=ones[:, :], compare_op=ALU.is_gt, fill=0.0,
                               base=0, pattern=[[-1, P]], channel_multiplier=1)
            pool.affine_select(out=earlier[:, 1, P:2 * P], in_=ones[:, :], compare_op=ALU.is_gt, fill=0.0,
                               base=0, pattern=[[-1, P]], channel_multiplier=1).then_inc(consts_ready, 1)
            for l in layers:
                pool.sem_inc(l.retired, AHEAD)

            def gather(l, t):
                s = t.slot(AHEAD)
                for a in range(PAIR):
                    pool.indirect_dma_start(gathered_rows[s][:, a, :], None, l.gather_from,
                                            bass.IndirectOffsetOnAxis(ap=gather_now[s][:, a:a + 1], axis=0)
                                            ).then_inc(l.gathered[s], 16)

            def scatter(l, t):
                for a in range(PAIR):
                    pool.indirect_dma_start(l.scatter_to,
                                            bass.IndirectOffsetOnAxis(ap=scatter_now[t.slot(AHEAD)][:, a:a + 1], axis=0),
                                            message[t.slot(2)][:, a, :], None, compute_op=ALU.add
                                            ).then_inc(l.scattered[t.slot(2)], 16)

            def step(l, t):
                pool.wait_ge(l.scatter_ready, t.n + 1)
                pool.wait_ge(l.message_ready, t.n + 3)
                pool.sem_inc(pool_gate, 1)
                scatter(l, t)
                if (t + AHEAD).below(GROUPS):
                    pool.wait_ge(l.gather_ready, t.n + AHEAD + 1)
                    pool.wait_ge(l.normed_ready, t.n + 1)
                    pool.sem_inc(pool_gate, 1)
                    gather(l, t + AHEAD)
                pool.wait_ge(l.scattered[t.slot(2)], (t.use(2) + 1) * (16 * PAIR))
                pool.sem_inc(l.retired, 1)

            for l in layers:
                for g in range(AHEAD):
                    pool.wait_ge(l.gather_ready, g + 1)
                    gather(l, Turn(0, 0, g))
                if l.n == 0:
                    pool.wait_ge(x1_copied, 16 * COPY_PIECES)
                    pool.wait_ge(dump_zeroed, 32)
                else:
                    pool.wait_ge(agg_zeroed, 16 * ZERO_PIECES)
                turns(pool, GROUPS, 2, AHEAD, lambda t: step(l, t))

        @block.scalar
        def _(act):
            act.wait_ge(wT_done, 1)
            act.activation(wT[:, :, :].rearrange("p k o -> p (k o)"), ps_a[:, 0, 0:KB * D], ACT.Copy).then_inc(wT_ready, 1)

            for l in layers:
                act.sem_inc(l.message_ready, 2)
            act.wait_ge(consts_ready, 2)

            def std(l, t):
                s = t.slot(2)
                act.wait_ge(l.moments_ready, t.n + 1)
                act.activation(row_std[s][:, :], row_moments[s][:, :, 1], ACT.Sqrt, bias=eps_col[:, :]).then_inc(l.std_ready, 1)

            def norm(l, t):
                s = t.slot(2)
                act.wait_ge(l.norm_ready, t.n + 1)
                act.wait_ge(l.summed if l.n == 0 else l.message_done, t.n + 1)
                for a in range(PAIR):
                    ins = act.activation(normed[s][:, a, :], gathered_rows[t.slot(AHEAD)][:, a, :], ACT.Relu,
                                         scale=row_norm[s][:, 0, a:a + 1], bias=row_norm[s][:, 1, a:a + 1])
                ins.then_inc(l.normed_ready, 1)

            def take_sums(l, t):
                s = t.slot(2)
                act.wait_ge(l.summed, t.n + 3)
                act.activation(summedT[s][:, :, :].rearrange("p k q -> p (k q)"), ps_a[:, 2 + s, :],
                               ACT.Copy).then_inc(l.summed_out, 1)

            def take_message(l, t):
                s = t.slot(2)
                act.wait_ge(l.message_done, t.n + 3)
                act.wait_ge(l.retired, t.n + AHEAD - 1)
                act.activation(message[s][:, :, :].rearrange("p a d -> p (a d)"), ps_b[:, s, :],
                               ACT.Copy).then_inc(l.message_ready, 1)

            def edges0(t):
                if t.below(GROUPS):
                    std(layers[0], t)
                if (t + -1).below(GROUPS):
                    take_sums(layers[0], t + -1)
                if t.below(GROUPS):
                    norm(layers[0], t)
                if (t + -2).below(GROUPS):
                    take_message(layers[0], t + -2)
            turns(act, GROUPS + 2, 2, 2, edges0)

            def edges1(t):
                if t.below(GROUPS):
                    std(layers[1], t)
                    norm(layers[1], t)
                if (t + -1).below(GROUPS):
                    take_message(layers[1], t + -1)
            turns(act, GROUPS + 1, 1, 2, edges1)

            act.wait_ge(stats_done, CHUNKS)
            act.activation(node_std[:, :, :], node_moments[:, :, :, 1], ACT.Sqrt, bias=eps_col[:, :]).then_inc(node_std_ready, 1)

            def relu_norm(c, s):
                p, j = shape_of(c)
                for r in range(j):
                    ins = act.activation(relu_ln[s][0:p, r, :], x1_in[s][0:p, r, :], ACT.Relu,
                                         scale=norm_now[s][0:p, 0, r:r + 1], bias=norm_now[s][0:p, 1, r:r + 1])
                return ins

            def gram_norm(c, s, k):
                act.wait_ge(norm_picked, c + 1)
                act.wait_ge(gram_x_loaded[s], 16 * k + 16)
                act.wait_ge(gram_h, c + 1)
                relu_norm(c, s).then_inc(gram_relu, 1)

            def gram(c, s, k):
                if not (isinstance(c, int) and c + 1 == CHUNKS):
                    gram_norm(c + 1, 1 - s, k if s == 0 else k + 1)
                act.wait_ge(gram_h, c + 3)
                act.wait_ge(gram_used, c + 1)
                p, j = shape_of(c)
                act.activation(gram_in[s][0:p, 0:j, 0, :], h[s][0:p, 0:j, :], ACT.Copy).then_inc(gram_hi, 1)
            gram_norm(0, 0, 0)
            chunk_schedule(act, gram)

            act.wait_ge(gram_used, CHUNKS + 2)
            act.activation(gram0[:, :], ps_a[:, 0, :], ACT.Copy)
            act.activation(gram1[:, :], ps_a[:, 1, 0:D + P], ACT.Copy).then_inc(bn_act, 1)

            act.wait_ge(bn_pe, 4)
            act.activation(bn_std[:, :], ps_b[:, 1, 0:MB], ACT.Sqrt, bias=eps_col[:, :]).then_inc(bn_act, 1)

            def prepare(n, s, k):
                act.wait_ge(norm_picked, CHUNKS + n + 1)
                act.wait_ge(main_loaded[s], 32 * k + 32)
                relu_norm(n, s).then_inc(ln_ready, 1)

            act.wait_ge(bn_ready, 1)
            prepare(0, 0, 0)

            def main(n, s, k):
                p, j = shape_of(n)
                w = p * j
                for kb in range(KB):
                    act.wait_ge(hT_done, KB * n + kb + 1)
                    act.activation(hT_hi[:, kb, 0:w], ps_a[:, kb, 0:w], ACT.Copy).then_inc(hT_hi_ready, 1)
                for m in range(MB):
                    act.wait_ge(up_done, MB * n + m + 1)
                    if m >= 2:
                        act.wait_ge(hid_lo_ready, MB * n + m - 1)
                    elif not (isinstance(n, int) and n == 0):
                        act.wait_ge(hid_lo_ready, MB * n + m - 1)
                    act.activation(hid[m % 2][:, 0:w], ps_a[:, 2 + m % 2, 0:w], ACT.Relu,
                                   scale=bn_scale[:, m:m + 1], bias=bn_bias[:, m:m + 1]).then_inc(hid_ready, 1)
                    if m >= 4 or not (isinstance(n, int) and n == 0):
                        act.wait_ge(down_done, MB * n + m - 3)
                    act.wait_ge(hid_ready, MB * n + m + 1)
                    act.activation(hid_hi[m % 4][:, 0:w], hid[m % 2][:, 0:w], ACT.Copy).then_inc(hid_hi_ready, 1)
                    if m == 4 and not (isinstance(n, int) and n == CHUNKS - 1):
                        prepare(n + 1, 1 - s, (k if s == 0 else k + 1))
            main_schedule(act, main)

        @block.vector
        def _(dve):
            class Chain:
                def __init__(self):
                    self.before, self.n = 0, 0

                def then(self, ins):
                    self.n += 1
                    ins.then_inc(dve_step, 1)

                def wait(self):
                    dve.wait_ge(dve_step, self.before + self.n)

            chain = Chain()

            def looped(count, per, body):
                start = chain.before + chain.n
                with dve.Fori(0, count) as i:
                    chain.before, chain.n = i * per + start, 0
                    body(i)
                    assert chain.n == per, chain.n
                chain.before, chain.n = start + count * per, 0

            dve.wait_ge(ids_loaded, 16 * 10)
            for n in range(2):
                view = lambda t: t[:, :].rearrange("p (g a) -> p g a", a=PAIR)
                chain.then(dve.tensor_copy(edge_info[n][:, :, 0:PAIR], view(target_ids[n])))
                chain.then(dve.tensor_copy(edge_info[n][:, :, PAIR:2 * PAIR], view(weights)))
                chain.then(dve.tensor_copy(edge_info[n][:, :, 2 * PAIR:3 * PAIR], view(dump_ids)))
                chain.wait()
                dve.tensor_tensor(edge_info[n][:, :, 2 * PAIR:3 * PAIR], edge_info[n][:, :, 2 * PAIR:3 * PAIR],
                                  edge_info[n][:, :, 0:PAIR], ALU.subtract).then_inc(info_built, 1)
            dve.wait_ge(info_built, 2)

            def pick_gather(l, t):
                dve.tensor_copy(gather_now[t.slot(AHEAD)][:, :],
                                l.gather_ids[:, bass.ds(t.n * PAIR, PAIR)]).then_inc(l.gather_ready, 1)

            def pick_info(l, t):
                dve.tensor_copy(info_now[t.slot(AHEAD)][:, :],
                                l.info[:, bass.ds(t.n, 1), :].rearrange("p g i -> p (g i)")).then_inc(l.info_ready, 1)

            def edge_step(l, t):
                s, s4 = t.slot(2), t.slot(AHEAD)
                info = info_now[s4]
                if (t + 1).below(GROUPS):
                    pick_info(l, t + 1)
                dve.wait_ge(l.gathered[s4], (t.use(AHEAD) + 1) * (16 * PAIR))
                for a in range(PAIR):
                    ins = dve.bn_stats(row_stats[:, a, :], gathered_rows[s4][:, a, :])
                chain.then(ins)
                chain.wait()
                if (t + AHEAD).below(GROUPS):
                    pick_gather(l, t + AHEAD)
                for a in range(PAIR):
                    ins = dve.bn_aggr(row_moments[s][:, a, :], row_stats[:, a, :])
                ins.then_inc(l.moments_ready, 1)
                dve.wait_ge(l.targets_spread, t.n + 1)
                dve.wait_ge(l.info_ready, t.n + 1)
                targets = ps_b[:, 2 + s, 0:PAIR * P]
                for a in range(PAIR):
                    upto = (a + 1) * P
                    ins = dve.scalar_tensor_tensor(same_earlier[:, a, 0:upto], targets[:, 0:upto], info[:, a:a + 1],
                                                   earlier[:, a, 0:upto], ALU.is_equal, ALU.mult,
                                                   accum_out=n_earlier[:, a:a + 1])
                chain.then(ins)
                dve.wait_ge(l.std_ready, t.n + 1)
                chain.then(dve.reciprocal(row_norm[s][:, 0, :], row_std[s][:, :]))
                chain.wait()
                dve.scalar_tensor_tensor(row_norm[s][:, 1, :], row_moments[s][:, :, 0], -1.0, row_norm[s][:, 0, :],
                                         ALU.mult, ALU.mult).then_inc(l.norm_ready, 1)
                for a in range(PAIR):
                    if l.n == 0:
                        ins = dve.tensor_scalar(same[s][:, a, :], targets, info[:, a:a + 1],
                                                info[:, PAIR + a:PAIR + a + 1], ALU.is_equal, ALU.mult)
                    else:
                        ins = dve.tensor_scalar(same[s][:, a, :], targets, info[:, a:a + 1], None, ALU.is_equal)
                ins.then_inc(l.same_ready, 1)
                chain.then(dve.scalar_tensor_tensor(shift[:, :], n_earlier[:, :], 0.0, info[:, 2 * PAIR:3 * PAIR],
                                                    ALU.is_gt, ALU.mult))
                chain.wait()
                dve.wait_ge(l.retired, t.n + 1)
                dve.tensor_tensor(scatter_now[s4][:, :], shift[:, :], info[:, 0:PAIR], ALU.add).then_inc(l.scatter_ready, 1)

            def node_step(c, s, k):
                p, j = shape_of(c)
                dve.wait_ge(stats_loaded[s], 16 * k + 16)
                for r in range(j):
                    ins = dve.bn_stats(node_stats[0:p, r, :], x1_in[s][0:p, r, :])
                chain.then(ins)
                chain.wait()
                dve.sem_inc(stats_taken, 1)
                for r in range(j):
                    ins = dve.bn_aggr(chunk_moments[0:p, r, :], node_stats[0:p, r, :])
                chain.then(ins)
                chain.wait()
                dve.tensor_copy(node_moments[0:p, bass.ds(c, 1), 0:j, :].rearrange("p c j t -> p (c j t)"),
                                chunk_moments[0:p, 0:j, :].rearrange("p j t -> p (j t)")).then_inc(stats_done, 1)

            dve.sem_inc(stats_taken, 2)
            dve.sem_inc(gram_h, 2)
            dve.sem_inc(gram_lo, 2)
            dve.wait_ge(consts_ready, 3)
            chain.then(dve.tensor_copy(ones_r[:, :], ones[:, :]))

            EDGE = 4
            NODE = 2
            for l in layers:
                if l.n == 1:
                    dve.wait_ge(w12_loaded, 16 * 6)
                    chain.then(dve.tensor_copy(w1_hi[:, :, :], w1_f[:, :, :]))
                    chain.then(dve.tensor_copy(w2_hl[:, :, 0, :], w2_f[:, :, :]))
                    chain.wait()
                    dve.tensor_tensor(w1_lo[:, :, :], w1_f[:, :, :], w1_hi[:, :, :].bitcast(F32), ALU.subtract)
                    dve.tensor_tensor(w2_hl[:, :, 1, :], w2_f[:, :, :], w2_hl[:, :, 0, :].bitcast(F32),
                                      ALU.subtract).then_inc(w12_split, 1)
                    dve.wait_ge(layers[0].retired, GROUPS + AHEAD)
                for g in range(AHEAD):
                    pick_gather(l, Turn(0, 0, g))
                pick_info(l, Turn(0, 0, 0))

                def edge_turn(t):
                    edge_step(l, t)
                    if l.n:
                        node_step(t.n, t.slot(2), t.use(2))
                turns(dve, GROUPS, 2, AHEAD, edge_turn,
                      loop=lambda passes, body: looped(passes, AHEAD * (EDGE + NODE * l.n), body))

            dve.wait_ge(node_std_ready, 1)
            chain.then(dve.reciprocal(node_rstd[:, :, :], node_std[:, :, :]))
            chain.wait()
            chain.then(dve.scalar_tensor_tensor(node_shift[:, :, :], node_moments[:, :, :, 0], -1.0, node_rstd[:, :, :],
                                                ALU.mult, ALU.mult))
            chain.wait()

            def pick_norm(c, s):
                dve.tensor_copy(norm_now[s][:, 0, :], node_rstd[:, bass.ds(c, 1), :].rearrange("p c j -> p (c j)"))
                dve.tensor_copy(norm_now[s][:, 1, :], node_shift[:, bass.ds(c, 1), :].rearrange("p c j -> p (c j)")).then_inc(norm_picked, 1)

            pick_norm(0, 0)
            pick_norm(1, 1)

            def gram_add(c, s, k):
                p, j = shape_of(c)
                dve.wait_ge(gram_relu, c + 1)
                dve.wait_ge(gram_a_loaded[s], 16 * k + 16)
                dve.wait_ge(gram_lo, c + 1)
                dve.tensor_tensor(h[s][0:p, 0:j, :], relu_ln[s][0:p, 0:j, :], agg_in[s][0:p, 0:j, :], ALU.add).then_inc(gram_h, 1)
                if not (isinstance(c, int) and c + 2 >= CHUNKS):
                    pick_norm(c + 2, s)

            def gram(c, s, k):
                p, j = shape_of(c)
                if not (isinstance(c, int) and c + 1 == CHUNKS):
                    gram_add(c + 1, 1 - s, k if s == 0 else k + 1)
                dve.wait_ge(gram_hi, c + 1)
                dve.tensor_tensor(gram_in[s][0:p, 0:j, 1, :], h[s][0:p, 0:j, :], gram_in[s][0:p, 0:j, 0, :].bitcast(F32),
                                  ALU.subtract).then_inc(gram_lo, 1)
            gram_add(0, 0, 0)
            chunk_schedule(dve, gram, single=4)
            pick_norm(0, 0)
            pick_norm(1, 1)

            dve.wait_ge(gram_used, CHUNKS + 2)
            chain.then(dve.tensor_scalar(gram_sum[:, :], ps_a[:, 2, 0:D], 1.0 / N, None, ALU.mult))
            chain.wait()
            dve.scalar_tensor_tensor(mu_row[:, :], ps_a[:, 2, D:2 * D], 1.0 / N, gram_sum[:, :], ALU.mult,
                                     ALU.add).then_inc(bn_act, 1)
            dve.wait_ge(bn_act, 2)
            chain.then(dve.tensor_tensor(cov[0][:, :], gram0[:, 0:D], gram0[:, D:2 * D], ALU.add))
            chain.then(dve.tensor_tensor(cov[1][:, P:D], gram1[:, 0:P], gram1[:, D:D + P], ALU.add))
            dve.wait_ge(bn_pe, 1)
            chain.wait()
            chain.then(dve.tensor_tensor(cov[0][:, :], cov[0][:, :], ps_b[:, 0, 0:D], ALU.add))
            chain.then(dve.tensor_tensor(cov[1][:, P:D], cov[1][:, P:D], ps_b[:, 0, D:D + P], ALU.add))
            chain.then(dve.tensor_scalar(mu_col[:, :], ps_b[:, 3, 0:KB], 1.0 / P, None, ALU.mult))
            chain.wait()
            chain.then(dve.scalar_tensor_tensor(cov[0][:, :], cov[0][:, :], 1.0 / N, ps_b[:, 1, 0:D], ALU.mult, ALU.subtract))
            dve.scalar_tensor_tensor(cov[1][:, P:D], cov[1][:, P:D], 1.0 / N, ps_b[:, 2, P:D], ALU.mult,
                                     ALU.subtract).then_inc(bn_act, 1)
            dve.wait_ge(bn_pe, 2)
            dve.tensor_copy(cov[1][:, 0:P], ps_b[:, 0, 0:P]).then_inc(bn_act, 1)
            dve.wait_ge(bn_pe, 3)
            for i in range(KB):
                ins = dve.tensor_tensor(w1_cov[:, i, :].rearrange("p (a n) -> p a n", a=2),
                                        w1_f[:, i, :].rearrange("p (a n) -> p a n", a=2),
                                        ps_a[:, 2 * i:2 * i + 2, :], ALU.mult)
            ins.then_inc(bn_act, 1)
            dve.wait_ge(bn_pe, 4)
            chain.then(dve.tensor_tensor(bn_mean[:, :], ps_b[:, 2, 0:MB], b1_v, ALU.add))
            dve.wait_ge(bn_act, 6)
            chain.then(dve.reciprocal(bn_scale[:, :], bn_std[:, :]))
            chain.wait()
            chain.then(dve.tensor_tensor(bn_scale[:, :], bn_scale[:, :], gamma_v, ALU.mult))
            chain.then(dve.tensor_tensor(bn_mean[:, :], b1_v, bn_mean[:, :], ALU.subtract))
            chain.wait()
            chain.then(dve.tensor_tensor(bn_bias[:, :], bn_scale[:, :], bn_mean[:, :], ALU.mult))
            chain.wait()
            dve.tensor_tensor(bn_bias[:, :], bn_bias[:, :], beta_v, ALU.add).then_inc(bn_ready, 1)

            def add_agg(n, s, k):
                p, j = shape_of(n)
                dve.wait_ge(ln_ready, n + 1)
                dve.wait_ge(main_loaded[s], 32 * k + 32)
                dve.tensor_tensor(h[s][0:p, 0:j, :], relu_ln[s][0:p, 0:j, :], agg_in[s][0:p, 0:j, :], ALU.add).then_inc(h_ready, 1)

            def read_down(n, s, k):
                p, j = shape_of(n)
                dve.wait_ge(down_done, MB * n + MB)
                dve.wait_ge(out_retired, n + 1)
                chain.then(dve.tensor_tensor(out_sb[s][0:p, 0:j, :], ps_b[0:p, 0:j, 0:D],
                                             b2_bc[0:p, :].rearrange("p (a d) -> p a d", a=1).to_broadcast([p, j, D]), ALU.add))
                chain.wait()
                dve.tensor_tensor(out_sb[s][0:p, 0:j, :], out_sb[s][0:p, 0:j, :], ps_b[0:p, 0:j, D:2 * D],
                                  ALU.add).then_inc(down_read, 1)

            def finish(n, s):
                p, j = shape_of(n)
                dve.wait_ge(down_read, n + 1)
                dve.scalar_tensor_tensor(out_sb[s][0:p, 0:j, :], out_sb[s][0:p, 0:j, :], 0.0, x1_in[s][0:p, 0:j, :],
                                         ALU.max, ALU.add).then_inc(out_ready, 1)

            add_agg(0, 0, 0)

            def main(n, s, k):
                p, j = shape_of(n)
                w = p * j
                first = isinstance(n, int) and n == 0
                for kb in range(KB):
                    dve.wait_ge(hT_hi_ready, KB * n + kb + 1)
                    dve.tensor_tensor(hT_lo[:, kb, 0:w], ps_a[:, kb, 0:w], hT_hi[:, kb, 0:w].bitcast(F32),
                                      ALU.subtract).then_inc(hT_lo_ready, 1)
                if not first:
                    read_down(n - 1, 1 - s, k)
                for m in range(MB):
                    dve.wait_ge(hid_hi_ready, MB * n + m + 1)
                    if m >= 4 or not first:
                        dve.wait_ge(down_done, MB * n + m - 3)
                    dve.tensor_tensor(hid_lo[m % 4][:, 0:w], hid[m % 2][:, 0:w], hid_hi[m % 4][:, 0:w].bitcast(F32),
                                      ALU.subtract).then_inc(hid_lo_ready, 1)
                    if m == 1 and not first:
                        finish(n - 1, 1 - s)
                    if m == 6 and not (isinstance(n, int) and n == CHUNKS - 1):
                        add_agg(n + 1, 1 - s, (k if s == 0 else k + 1))
                    if m == 2 and not (isinstance(n, int) and n + 2 >= CHUNKS):
                        pick_norm(n + 2, s)
            main(0, 0, 0)
            def pair(i):
                main(2 * i + 1, 1, i)
                main(2 * i + 2, 0, i + 1)
            looped(MAIN_PAIRS, 2, pair)
            for n in range(CHUNKS - 3, CHUNKS):
                main(n, n % 2, n // 2)
            read_down(CHUNKS - 1, (CHUNKS - 1) % 2, (CHUNKS - 1) // 2)
            finish(CHUNKS - 1, (CHUNKS - 1) % 2)

        @block.tensor
        def _(pe):
            for l in layers:
                pe.sem_inc(l.message_done, 2)
                pe.sem_inc(l.same_ready, 2)
            pe.sem_inc(layers[0].summed, 2)
            pe.sem_inc(gram_used, 2)
            pe.wait_ge(consts_ready, 3)
            pe.wait_ge(w_loaded, 16)
            for k in range(KB):
                for o in range(KB):
                    ins = pe.transpose(ps_a[:, 0, k * D + o * P:k * D + (o + 1) * P], w_rows[:, o, k * P:(k + 1) * P], ident[:, :])
            ins.then_inc(wT_done, 1)
            pe.wait_ge(wT_ready, 1)

            def spread(l, t):
                s = t.slot(2)
                pe.wait_ge(l.info_ready, t.n + 1)
                pe.wait_ge(l.same_ready, t.n + 1)
                for b in range(PAIR):
                    ins = pe.transpose(ps_b[:, 2 + s, b * P:(b + 1) * P],
                                       info_now[t.slot(AHEAD)][:, b:b + 1].to_broadcast([P, P]), ident[:, :])
                ins.then_inc(l.targets_spread, 1)

            def sum_rows(l, t):
                s = t.slot(2)
                pe.wait_ge(l.same_ready, t.n + 3)
                pe.wait_ge(l.normed_ready, t.n + 1)
                for kb in range(KB):
                    for a in range(PAIR):
                        ins = pe.matmul(ps_a[:, 2 + s, kb * PAIR * P:(kb + 1) * PAIR * P],
                                        normed[s][:, a, kb * P:(kb + 1) * P], same[s][:, a, :],
                                        start=(a == 0), stop=(a == PAIR - 1))
                ins.then_inc(l.summed, 1)

            def multiply(l, t):
                s = t.slot(2)
                pe.wait_ge(l.summed_out, t.n + 1)
                pe.wait_ge(l.message_ready, t.n + 1)
                for b in range(PAIR):
                    for kb in range(KB):
                        ins = pe.matmul(ps_b[:, s, b * D:(b + 1) * D], summedT[s][:, kb, b * P:(b + 1) * P],
                                        wT[:, kb, :], start=(kb == 0), stop=(kb == KB - 1))
                ins.then_inc(l.message_done, 1)

            def sum_messages(l, t):
                s = t.slot(2)
                pe.wait_ge(l.same_ready, t.n + 3)
                pe.wait_ge(l.normed_ready, t.n + 1)
                pe.wait_ge(l.message_ready, t.n + 1)
                for b in range(PAIR):
                    for a in range(PAIR):
                        ins = pe.matmul(ps_b[:, s, b * D:(b + 1) * D], same[s][:, a, b * P:(b + 1) * P],
                                        normed[s][:, a, :], start=(a == 0), stop=(a == PAIR - 1))
                ins.then_inc(l.message_done, 1)

            def edges0(t):
                if (t + 1).below(GROUPS):
                    spread(layers[0], t + 1)
                if (t + -1).below(GROUPS):
                    multiply(layers[0], t + -1)
                if t.below(GROUPS):
                    sum_rows(layers[0], t)

            def edges1(t):
                if (t + 1).below(GROUPS):
                    spread(layers[1], t + 1)
                sum_messages(layers[1], t)

            spread(layers[0], Turn(0, 0, 0))
            turns(pe, GROUPS + 1, 1, 2, edges0)
            spread(layers[1], Turn(0, 0, 0))
            turns(pe, GROUPS, 1, 1, edges1)

            def gram(c, s, k):
                p, j = shape_of(c)
                pe.wait_ge(gram_lo, c + 3)
                for r in range(j):
                    first = isinstance(c, int) and c == 0 and r == 0
                    last = isinstance(c, int) and c == CHUNKS - 1 and r == j - 1
                    both = gram_in[s][0:p, r, :, :].rearrange("p t d -> p (t d)")
                    pe.matmul(ps_a[:, 0, :], both[:, 0:P], both, start=first, stop=last)
                    pe.matmul(ps_a[:, 1, 0:D + P], both[:, P:D], both[:, P:2 * D], start=first, stop=last)
                    ins = pe.matmul(ps_a[:, 2, :], ones_r[0:p, :], both, start=first, stop=last)
                ins.then_inc(gram_used, 1)
            gram(0, 0, 0)
            gram(1, 1, 0)
            with pe.Fori(0, FULL_CHUNKS // 2 - 1) as i:
                gram(2 * i + 2, 0, i + 1)
                gram(2 * i + 3, 1, i + 1)
            for c in range(FULL_CHUNKS // 2 * 2, CHUNKS):
                gram(c, c % 2, c // 2)

            pe.wait_ge(bn_act, 2)
            pe.transpose(ps_b[:, 0, 0:P], gram0[:, D:D + P], ident[:, :])
            pe.transpose(ps_b[:, 0, P:D], gram1[:, P:D], ident[:, :])
            pe.transpose(ps_b[:, 0, D:D + P], gram1[:, D:D + P], ident[:, :])
            for k in range(KB):
                pe.matmul(ps_b[:, 1 + k, 0:D], mu_row[0:1, k * P:(k + 1) * P], mu_row[0:1, :], start=True, stop=True)
            for k in range(KB):
                ins = pe.matmul(ps_b[:, 3, k:k + 1], mu_row[:, k * P:(k + 1) * P], ones[:, 0:1], start=True, stop=True)
            ins.then_inc(bn_pe, 1)
            pe.wait_ge(bn_act, 3)
            pe.transpose(ps_b[:, 0, 0:P], cov[0][:, P:D], ident[:, :]).then_inc(bn_pe, 1)
            pe.wait_ge(bn_act, 4)
            for i in range(KB):
                for a in range(2):
                    for k in range(KB):
                        ins = pe.matmul(ps_a[:, 2 * i + a, :], cov[k][:, i * P:(i + 1) * P], w1_f[:, k, a * 512:(a + 1) * 512],
                                        start=(k == 0), stop=(k == KB - 1))
            ins.then_inc(bn_pe, 1)
            pe.wait_ge(bn_act, 5)
            for m in range(MB):
                for i in range(KB):
                    pe.matmul(ps_b[:, 1, m:m + 1], w1_cov[:, i, m * P:(m + 1) * P], ones[:, 0:1],
                              start=(i == 0), stop=(i == KB - 1))
                for k in range(KB):
                    ins = pe.matmul(ps_b[:, 2, m:m + 1], w1_f[:, k, m * P:(m + 1) * P], mu_col[:, k:k + 1],
                                    start=(k == 0), stop=(k == KB - 1))
            ins.then_inc(bn_pe, 1)
            pe.wait_ge(bn_ready, 1)
            pe.wait_ge(w12_split, 1)

            def transpose_h(n, s):
                p, j = shape_of(n)
                pe.wait_ge(h_ready, n + 1)
                for kb in range(KB):
                    for r in range(j):
                        ins = pe.transpose(ps_a[:, kb, r * p:(r + 1) * p], h[s][0:p, r, kb * P:(kb + 1) * P], ident[0:p, 0:p])
                    ins.then_inc(hT_done, 1)

            def up(n, m):
                p, j = shape_of(n)
                w = p * j
                if m == 0:
                    pe.wait_ge(hT_hi_ready, KB * n + KB)
                    pe.wait_ge(hT_lo_ready, KB * n + KB)
                if m >= 2 or not (isinstance(n, int) and n == 0):
                    pe.wait_ge(hid_ready, MB * n + m - 1)
                cols = slice(m * P, (m + 1) * P)
                terms = [(w_part, h_part, kb) for kb in range(KB)
                         for w_part, h_part in ((w1_hi, hT_hi), (w1_hi, hT_lo), (w1_lo, hT_hi))]
                for t, (w_part, h_part, kb) in enumerate(terms):
                    ins = pe.matmul(ps_a[:, 2 + m % 2, 0:w], w_part[:, kb, cols], h_part[:, kb, 0:w],
                                    start=(t == 0), stop=(t == len(terms) - 1))
                ins.then_inc(up_done, 1)

            def down(n, m):
                p, j = shape_of(n)
                pe.wait_ge(hid_hi_ready, MB * n + m + 1)
                pe.wait_ge(hid_lo_ready, MB * n + m + 1)
                if m == 0 and not (isinstance(n, int) and n == 0):
                    pe.wait_ge(down_read, n)
                w2 = w2_hl[:, m, :, :].rearrange("p t d -> p (t d)")
                for r in range(j):
                    cols = slice(r * p, (r + 1) * p)
                    pe.matmul(ps_b[0:p, r, :], hid_hi[m % 4][:, cols], w2, start=(m == 0), stop=(m == MB - 1), skip_group_check=True)
                    ins = pe.matmul(ps_b[0:p, r, 0:D], hid_lo[m % 4][:, cols], w2[:, 0:D], start=False, stop=(m == MB - 1), skip_group_check=True)
                ins.then_inc(down_done, 1)

            def main(n, s, k):
                transpose_h(n, s)
                if not (isinstance(n, int) and n == 0):
                    down(n - 1, MB - 2)
                    down(n - 1, MB - 1)
                up(n, 0)
                up(n, 1)
                for m in range(2, MB):
                    up(n, m)
                    down(n, m - 2)
            main_schedule(pe, main)
            down(CHUNKS - 1, MB - 2)
            down(CHUNKS - 1, MB - 1)


def kernel(x, src, dst, edge_weight, L0_gnn_W, L1_gnn_W1, L1_gnn_b1, L1_gnn_gamma, L1_gnn_beta, L1_gnn_W2, L1_gnn_b2):
    import numpy as np
    import concourse.bacc as bacc
    from concourse import mybir
    from concourse.bass_utils import run_bass_kernel_spmd

    nc = bacc.Bacc("TRN2", target_bir_lowering=False, num_devices=1)
    given = dict(x=x, src=src, dst=dst, edge_weight=edge_weight, W=L0_gnn_W, W1=L1_gnn_W1, b1=L1_gnn_b1,
                 gamma=L1_gnn_gamma, beta=L1_gnn_beta, W2=L1_gnn_W2, b2=L1_gnn_b2)
    arrays = {f"in_{name}": np.ascontiguousarray(a) for name, a in given.items()}
    aps = {name: nc.dram_tensor(f"in_{name}", arrays[f"in_{name}"].shape,
                                mybir.dt.from_np(arrays[f"in_{name}"].dtype), kind="ExternalInput").ap()
           for name in given}
    out = nc.dram_tensor("out", arrays["in_x"].shape, mybir.dt.float32, kind="ExternalOutput").ap()
    gnn_program(nc, out=out, **aps)
    result = run_bass_kernel_spmd(nc, [arrays], core_ids=[0])
    return result.results[0]["out"]
```

```python
def gnn_program(nc, x, src, dst, edge_weight, W, W1, b1, gamma, beta, W2, b2, out):
    from contextlib import ExitStack

    import concourse.bass as bass
    from concourse import mybir

    F32, F32R, I32 = mybir.dt.float32, mybir.dt.float32r, mybir.dt.int32
    ALU = mybir.AluOpType
    ACT = mybir.ActivationFunctionType

    P = 128
    N, D = x.shape
    E = src.shape[0]
    HID = W1.shape[1]
    KB = D // P
    MB = HID // P
    EPS = 1e-5

    QUAD = 4
    COLS = -(-E // (P * QUAD)) * QUAD
    GROUPS = COLS // QUAD
    FULL_EDGE_ROWS = E // COLS
    LAST_EDGES = E - FULL_EDGE_ROWS * COLS
    assert FULL_EDGE_ROWS == P - 1
    DUMP_ROWS = P * QUAD
    AHEAD = 4

    ROWS = 4
    CHUNK = P * ROWS
    FULL_CHUNKS = N // CHUNK
    TAIL_NODES = N - FULL_CHUNKS * CHUNK
    TAIL_ROWS = 3
    TAIL_P = TAIL_NODES // TAIL_ROWS
    assert TAIL_P * TAIL_ROWS == TAIL_NODES and TAIL_P <= P and TAIL_P % 16 == 0
    CHUNKS = FULL_CHUNKS + 1
    assert CHUNKS == 2 * GROUPS

    ZERO_PIECES = 40
    ZERO_LEN = N * D // ZERO_PIECES // P
    assert ZERO_PIECES * P * ZERO_LEN == N * D and ZERO_LEN >= DUMP_ROWS * D // P and ZERO_PIECES + AHEAD + 1 <= GROUPS
    COPY_PIECES = 10
    COPY_PARTS = 400
    assert N * D % (COPY_PIECES * COPY_PARTS) == 0

    x1_table = nc.dram_tensor("x1_table", (N + DUMP_ROWS, D), F32, kind="Internal").ap()
    agg_table = nc.dram_tensor("agg_table", (N + DUMP_ROWS, D), F32, kind="Internal").ap()

    def full_chunks(table):
        return table[0:FULL_CHUNKS * CHUNK, :].rearrange("(c p j) d -> c p (j d)", p=P, j=ROWS)

    def tail_chunk(table):
        return table[FULL_CHUNKS * CHUNK:N, :].rearrange("(p j) d -> p (j d)", j=TAIL_ROWS)

    with ExitStack() as ctx:
        def sb(name, shape, dt=F32):
            return ctx.enter_context(nc.sbuf_tensor(name, shape, dt))

        def sem(name):
            return ctx.enter_context(nc.semaphore(name))

        ident = sb("ident", [P, P])
        ones = sb("ones", [P, P])
        ones_r = sb("ones_r", [P, P], F32R)
        zeros = sb("zeros", [P, ZERO_LEN])
        eps_col = sb("eps_col", [P, 1])
        before = sb("before", [P, P])
        gather_ids = [sb(f"gather_ids{i}", [P, COLS], I32) for i in range(2)]
        target_ids = [sb(f"target_ids{i}", [P, COLS], I32) for i in range(2)]
        dump_ids = sb("dump_ids", [P, COLS], I32)
        weights = sb("weights", [P, COLS])
        edge_info = [sb(f"edge_info{i}", [P, GROUPS, 3 * QUAD]) for i in range(2)]
        info_now = [sb(f"info_now{s}", [P, 3 * QUAD]) for s in range(AHEAD)]
        gather_now = [sb(f"gather_now{s}", [P, QUAD], I32) for s in range(AHEAD)]
        scatter_now = [sb(f"scatter_now{s}", [P, QUAD], I32) for s in range(AHEAD)]
        row_norm = [sb(f"row_norm{s}", [P, 2, QUAD]) for s in range(2)]
        row_stats = sb("row_stats", [P, QUAD, 6])
        row_moments = [sb(f"row_moments{s}", [P, QUAD, 2]) for s in range(2)]
        row_std = [sb(f"row_std{s}", [P, QUAD]) for s in range(2)]
        shift = sb("shift", [P, QUAD])
        node_stats = [sb(f"node_stats{s}", [P, ROWS, 6]) for s in range(2)]
        chunk_moments = [sb(f"chunk_moments{s}", [P, ROWS, 2]) for s in range(2)]
        node_moments = sb("node_moments", [P, CHUNKS, ROWS, 2])
        node_rstd = sb("node_rstd", [P, CHUNKS, ROWS])
        node_std = sb("node_std", [P, CHUNKS, ROWS])
        node_shift = sb("node_shift", [P, CHUNKS, ROWS])
        norm_now = [sb(f"norm_now{s}", [P, 2, ROWS]) for s in range(2)]
        w_rows = sb("w_rows", [P, KB, D])
        wT_hi = sb("wT_hi", [P, KB, D], F32R)
        wT_lo = sb("wT_lo", [P, KB, D], F32R)
        w1_f = sb("w1_f", [P, KB, HID])
        w1_hi = sb("w1_hi", [P, KB, HID], F32R)
        w1_lo = sb("w1_lo", [P, KB, HID], F32R)
        w2_f = sb("w2_f", [P, MB, D])
        w2_hl = sb("w2_hl", [P, MB, 2, D], F32R)
        b2_bc = sb("b2_bc", [P, D])
        hid_vec = sb("hid_vec", [P, 3, MB])
        b1_v, gamma_v, beta_v = (hid_vec[:, i, :] for i in range(3))
        gram0 = sb("gram0", [P, 2 * D])
        gram_sum = sb("gram_sum", [P, D])
        gram1 = sb("gram1", [P, D + P])
        mu_row = sb("mu_row", [P, D])
        mu_col = sb("mu_col", [P, KB])
        cov = [sb(f"cov{k}", [P, D]) for k in range(KB)]
        w1_cov = w2_f[:, :, :].rearrange("p m d -> p (m d)").rearrange("p (k n) -> p k n", k=KB)
        bn_scale = sb("bn_scale", [P, MB])
        bn_std = sb("bn_std", [P, MB])
        bn_bias = sb("bn_bias", [P, MB])
        bn_mean = sb("bn_mean", [P, MB])

        def carve(arena, start, *shape):
            size = 1
            for n in shape:
                size *= n
            names = "abc"[:len(shape)]
            flat = arena[:, start:start + size]
            tile = flat.rearrange(f"p ({' '.join(names)}) -> p {' '.join(names)}", **dict(zip(names, shape))) if len(shape) > 1 else flat
            return tile, start + size

        def carve_all(arena, *shapes):
            tiles, at = [], 0
            for shape in shapes:
                tile, at = carve(arena, at, *shape)
                tiles.append(tile)
            return tiles

        ARENA = 9728
        ARENA_R = 11264
        arena = sb("arena", [P, ARENA])
        arena_r = sb("arena_r", [P, ARENA_R], F32R)
        LOADS = 4
        x1_in = [sb(f"x1_in{s}", [P, ROWS, D]) for s in range(LOADS)]
        edge_tiles = carve_all(arena, *[(QUAD, D)] * (AHEAD + 4), *[(QUAD * P,)] * 3)
        gathered_rows = edge_tiles[0:AHEAD]
        normed = edge_tiles[AHEAD:AHEAD + 2]
        message = edge_tiles[AHEAD + 2:AHEAD + 4]
        targets_sb = edge_tiles[AHEAD + 4:AHEAD + 6]
        same0, same1, rows_hi0, rows_hi1, rows_lo0, rows_lo1, summed_hi, summed_lo, same_before0, same_before1 = carve_all(
            arena_r, *[(QUAD, QUAD * P)] * 2, *[(QUAD, D)] * 4, *[(KB, QUAD * P)] * 2, *[(QUAD, P)] * 2)
        rows_hi, rows_lo, same_before = [rows_hi0, rows_hi1], [rows_lo0, rows_lo1], [same_before0, same_before1]
        same = [same0, same1]
        same_diagonal = [arena_r[:, s * QUAD * QUAD * P:][:, 0:QUAD * (QUAD + 1) * P].rearrange(
            "p (a x) -> p a x", a=QUAD)[:, :, 0:P] for s in range(2)]
        node_tiles = carve_all(arena, *[(ROWS, D)] * (LOADS + 4), *[(CHUNK,)] * 2)
        agg_in = node_tiles[0:LOADS]
        relu_ln = node_tiles[LOADS:LOADS + 2]
        h = node_tiles[LOADS + 2:LOADS + 4]
        hid = node_tiles[LOADS + 4:LOADS + 6]
        gram_in = carve_all(arena_r, *[(ROWS, 2, D)] * 2)
        node_r = carve_all(arena_r, *[(KB, CHUNK)] * 2, *[(CHUNK,)] * 8)
        hT_hi, hT_lo = node_r[0:2]
        hid_hi, hid_lo = node_r[2:6], node_r[6:10]
        out_sb = [zeros[:, s * ROWS * D:(s + 1) * ROWS * D].rearrange("p (j d) -> p j d", j=ROWS) for s in range(2)]

        ps_a = ctx.enter_context(nc.psum_tensor("ps_a", [P, 4, 512], F32))
        ps_b = ctx.enter_context(nc.psum_tensor("ps_b", [P, 4, 512], F32))

        counts = ps_a[:, 1, 0:QUAD * 2].rearrange("p (b t) -> p b t", t=2)[:, :, 0]

        ids_blank = sem("ids_blank")
        consts_ready = sem("consts_ready")
        ids_loaded = sem("ids_loaded")
        w_loaded = sem("w_loaded")
        w12_loaded = sem("w12_loaded")
        x1_copied = [sem(f"x1_copied{s}") for s in range(2)]
        dump_zeroed = sem("dump_zeroed")
        agg_zeroed = sem("agg_zeroed")
        info_built = sem("info_built")
        wT_done = sem("wT_done")
        wT_ready = sem("wT_ready")
        dve_step = sem("dve_step")
        pool_gate = sem("pool_gate")

        class Layer:
            def __init__(self, n):
                self.n = n
                self.gather_from = (x, x1_table)[n]
                self.scatter_to = (x1_table, agg_table)[n]
                self.gather_ids = gather_ids[1 - n]
                self.info = edge_info[n]
                self.info_ready = sem(f"info_ready_L{n}")
                self.gather_ready = sem(f"gather_ready_L{n}")
                self.gathered = [sem(f"gathered_L{n}_{s}") for s in range(AHEAD)]
                self.moments_ready = sem(f"moments_ready_L{n}")
                self.std_ready = sem(f"std_ready_L{n}")
                self.norm_ready = sem(f"norm_ready_L{n}")
                self.normed_ready = sem(f"normed_ready_L{n}")
                self.rows_hi_ready = sem(f"rows_hi_ready_L{n}")
                self.rows_lo_ready = sem(f"rows_lo_ready_L{n}")
                self.targets_spread = sem(f"targets_spread_L{n}")
                self.targets_ready = sem(f"targets_ready_L{n}")
                self.same_ready = sem(f"same_ready_L{n}")
                self.before_ready = sem(f"before_ready_L{n}")
                self.counted = sem(f"counted_L{n}")
                self.scatter_ready = sem(f"scatter_ready_L{n}")
                self.summed = sem(f"summed_L{n}")
                self.sums_hi_ready = sem(f"sums_hi_ready_L{n}")
                self.sums_lo_ready = sem(f"sums_lo_ready_L{n}")
                self.message_done = sem(f"message_done_L{n}")
                self.message_ready = sem(f"message_ready_L{n}")
                self.scattered = [sem(f"scattered_L{n}_{s}") for s in range(2)]
                self.retired = sem(f"retired_L{n}")

        layers = [Layer(0), Layer(1)]

        stats_loaded = [sem(f"stats_loaded{s}") for s in range(2)]
        stats_taken = sem("stats_taken")
        stats_done = sem("stats_done")
        node_std_ready = sem("node_std_ready")
        gram_x_loaded = [sem(f"gram_x_loaded{s}") for s in range(LOADS)]
        gram_a_loaded = [sem(f"gram_a_loaded{s}") for s in range(LOADS)]
        norm_picked = sem("norm_picked")
        gram_relu = sem("gram_relu")
        gram_h = sem("gram_h")
        gram_hi = sem("gram_hi")
        gram_lo = sem("gram_lo")
        gram_used = sem("gram_used")
        bn_pe = sem("bn_pe")
        bn_act = sem("bn_act")
        bn_ready = sem("bn_ready")
        w12_split = sem("w12_split")

        main_loaded = [sem(f"main_loaded{s}") for s in range(LOADS)]
        ln_ready = sem("ln_ready")
        h_ready = sem("h_ready")
        hT_done = sem("hT_done")
        hT_hi_ready = sem("hT_hi_ready")
        hT_lo_ready = sem("hT_lo_ready")
        up_done = sem("up_done")
        hid_ready = sem("hid_ready")
        hid_hi_ready = sem("hid_hi_ready")
        hid_lo_ready = sem("hid_lo_ready")
        down_half = sem("down_half")
        down_done = sem("down_done")
        down_read = sem("down_read")
        out_ready = sem("out_ready")
        out_stored = [sem(f"out_stored{s}") for s in range(2)]
        out_retired = sem("out_retired")

        block = ctx.enter_context(nc.Block())

        class Turn:
            def __init__(self, i, per, base):
                self.i, self.per, self.base = i, per, base

            def __add__(self, d):
                return Turn(self.i, self.per, self.base + d)

            @property
            def n(self):
                return self.i * self.per + self.base if self.per else self.base

            def slot(self, slots):
                assert self.per % slots == 0
                return self.base % slots

            def use(self, slots):
                return self.i * (self.per // slots) + self.base // slots if self.per else self.base // slots

            def n_above(self, least):
                return self.per > 0 or self.base > least

            def below(self, end):
                return self.per > 0 or 0 <= self.base < end

        def turns(eng, total, head, tail, step, loop=None):
            for t in range(head):
                step(Turn(0, 0, t))
            passes = (total - head - tail) // AHEAD

            def body(i):
                for u in range(AHEAD):
                    step(Turn(i, AHEAD, head + u))
            if loop:
                loop(passes, body)
            else:
                with eng.Fori(0, passes) as i:
                    body(i)
            for t in range(head + passes * AHEAD, total):
                step(Turn(0, 0, t))

        assert LOADS == 4
        MAIN_PASSES = (CHUNKS - 1 - 3) // LOADS

        def shape_of(n):
            return (TAIL_P, TAIL_ROWS) if isinstance(n, int) and n == CHUNKS - 1 else (P, ROWS)

        def halves(j):
            return range(0, 2), range(2, j)

        def main_schedule(eng, step, loop=None):
            step(0, 0, 0)

            def body(i):
                for u in range(1, LOADS + 1):
                    step(LOADS * i + u, u % LOADS, i + u // LOADS)
            if loop:
                loop(MAIN_PASSES, body)
            else:
                with eng.Fori(0, MAIN_PASSES) as i:
                    body(i)
            for n in range(MAIN_PASSES * LOADS + 1, CHUNKS):
                step(n, n % LOADS, n // LOADS)

        def chunk_schedule(eng, step, single=2):
            with eng.Fori(0, (CHUNKS - single) // 2) as i:
                step(2 * i, 0, i)
                step(2 * i + 1, 1, i)
            for c in range(CHUNKS - single, CHUNKS):
                step(c, c % 2, c // 2)

        def chunk_of(table, c):
            if isinstance(c, int) and c == CHUNKS - 1:
                return tail_chunk(table)
            return full_chunks(table)[bass.ds(c, 1), :, :].rearrange("c p e -> p (c e)")

        def tile_of(tile, c):
            p, j = shape_of(c)
            return tile[0:p, 0:j, :].rearrange("p j d -> p (j d)")

        @block.sync
        def _(sp):
            sp.sem_inc(out_retired, 2)
            def pieces(table):
                return table[0:N, :].rearrange("n d -> (n d)").rearrange("(i a e) -> i a e", i=COPY_PIECES, a=COPY_PARTS)

            def copy_piece(i):
                if i >= 2:
                    sp.wait_ge(x1_copied[i % 2], 16 * (i // 2))
                sp.dma_start(pieces(x1_table)[i], pieces(x)[i]).then_inc(x1_copied[i % 2], 16)
            copy_piece(0)
            sp.wait_ge(ids_blank, 1)
            def load_edges(tile, ids):
                sp.dma_start(tile[0:FULL_EDGE_ROWS, :],
                             ids[0:FULL_EDGE_ROWS * COLS].rearrange("(p c) -> p c", c=COLS)).then_inc(ids_loaded, 16)
                sp.dma_start(tile[FULL_EDGE_ROWS:P, 0:LAST_EDGES],
                             ids[FULL_EDGE_ROWS * COLS:E].rearrange("(p c) -> p c", p=1)).then_inc(ids_loaded, 16)
            for i, ids in ((1, dst), (0, src)):
                load_edges(gather_ids[i], ids)
                load_edges(target_ids[i], ids)
            load_edges(weights, edge_weight)
            sp.dma_start(w_rows[:, :, :], W.rearrange("(b p) i -> p b i", p=P)).then_inc(w_loaded, 16)
            sp.wait_ge(consts_ready, 1)
            for table in (x1_table, agg_table):
                sp.dma_start(table[N:N + DUMP_ROWS, :].rearrange("(p j) d -> p (j d)", p=P),
                             zeros[:, 0:QUAD * D]).then_inc(dump_zeroed, 16)
            for i in range(1, COPY_PIECES):
                copy_piece(i)

            agg_pieces = agg_table[0:N, :].rearrange("n d -> (n d)").rearrange("(i p e) -> i p e", i=ZERO_PIECES, p=P)

            def zero_piece(i):
                sp.wait_ge(layers[0].normed_ready, i + AHEAD + 2)
                sp.dma_start(agg_pieces[bass.ds(i, 1), :, :].rearrange("i p e -> p (i e)"), zeros[:, :]).then_inc(agg_zeroed, 16)
            def load_w1():
                sp.dma_start(w1_f[:, :, :], W1.rearrange("(k p) n -> p k n", p=P)).then_inc(w12_loaded, 16)

            def load_w2():
                sp.dma_start(w2_f[:, :, :], W2.rearrange("(m p) n -> p m n", p=P)).then_inc(w12_loaded, 16)

            def load_vectors():
                sp.dma_start(b2_bc[:, :], b2.rearrange("(a n) -> a n", a=1).to_broadcast([P, D])).then_inc(w12_loaded, 16)
                with nc.allow_non_contiguous_dma(reason="three vectors of HID values, once"):
                    for i, v in enumerate((b1, gamma, beta)):
                        sp.dma_start(hid_vec[:, i, :], v.rearrange("(m p) -> p m", p=P)).then_inc(w12_loaded, 16)

            BETWEEN = ZERO_PIECES // 4
            for part, load in enumerate((load_w1, load_w2, load_vectors, None)):
                with sp.Fori(part * BETWEEN, (part + 1) * BETWEEN) as i:
                    zero_piece(i)
                if load:
                    load()

            sp.wait_ge(layers[0].retired, GROUPS + AHEAD)

            def load_stats(c, s, k):
                sp.wait_ge(stats_taken, c + 1)
                sp.dma_start(tile_of(x1_in[s], c), chunk_of(x1_table, c)).then_inc(stats_loaded[s], 16)
            chunk_schedule(sp, load_stats)

            sp.wait_ge(stats_taken, CHUNKS + 2)

            def load_gram_x(t):
                s = t.slot(LOADS)
                sp.dma_start(tile_of(x1_in[s], t.n), chunk_of(x1_table, t.n)).then_inc(gram_x_loaded[s], 16)

            def load_gram_agg(t):
                s = t.slot(LOADS)
                sp.dma_start(tile_of(agg_in[s], t.n), chunk_of(agg_table, t.n)).then_inc(gram_a_loaded[s], 16)

            def load_gram(t):
                if t.n_above(LOADS - 1):
                    sp.wait_ge(gram_h, t.n + 1)
                    load_gram_x(t)
                load_gram_agg(t)
            for c in range(LOADS):
                load_gram_x(Turn(0, 0, c))
            sp.wait_ge(layers[1].retired, GROUPS + AHEAD)
            turns(sp, CHUNKS, LOADS, 4, load_gram)
            sp.wait_ge(gram_h, CHUNKS + LOADS)

            def load_main(n, s):
                sp.dma_start(tile_of(x1_in[s], n), chunk_of(x1_table, n)).then_inc(main_loaded[s], 16)
                sp.dma_start(tile_of(agg_in[s], n), chunk_of(agg_table, n)).then_inc(main_loaded[s], 16)

            def load_and_store(n, s4, k, load=True):
                s = s4 % 2
                sp.wait_ge(out_ready, n + 1)
                if load:
                    load_main(n + LOADS, s4)
                sp.dma_start(chunk_of(out, n), tile_of(out_sb[s], n)).then_inc(out_stored[s], 16)
                sp.wait_ge(out_stored[s], 16 * k + 16)
                sp.sem_inc(out_retired, 1)

            for n in range(LOADS):
                load_main(n, n)
            STORE_PASSES = (CHUNKS - LOADS - 1) // LOADS
            with sp.Fori(0, STORE_PASSES) as i:
                for u in range(LOADS):
                    load_and_store(LOADS * i + u, u, 2 * i + u // 2)
            for n in range(STORE_PASSES * LOADS, CHUNKS):
                load_and_store(n, n % LOADS, n // 2, load=n + LOADS < CHUNKS)

        @block.gpsimd
        def _(pool):
            dump_pattern = [[0, GROUPS], [1, QUAD]]
            for t in (dump_ids, target_ids[0], target_ids[1]):
                pool.iota(t[:, :], pattern=dump_pattern, base=N, channel_multiplier=QUAD)
            pool.memset(gather_ids[0][:, :], 0)
            pool.memset(gather_ids[1][:, :], 0)
            pool.memset(weights[:, :], 0.0).then_inc(ids_blank, 1)
            pool.memset(zeros[:, :], 0.0).then_inc(consts_ready, 1)
            pool.memset(node_moments[:, :, :, :], 1.0)
            pool.memset(eps_col[:, :], EPS)
            pool.memset(ident[:, :], 0.0)
            pool.memset(ones[:, :], 1.0).then_inc(consts_ready, 1)
            pool.wait_ge(consts_ready, 2)
            pool.affine_select(out=ident[:, :], in_=ident[:, :], compare_op=ALU.not_equal, fill=1.0,
                               base=0, pattern=[[-1, P]], channel_multiplier=1)
            pool.affine_select(out=before[:, :], in_=ones[:, :], compare_op=ALU.is_gt, fill=0.0,
                               base=0, pattern=[[1, P]], channel_multiplier=-1).then_inc(consts_ready, 1)
            for l in layers:
                pool.sem_inc(l.retired, AHEAD)

            def gather(l, t):
                s = t.slot(AHEAD)
                for a in range(QUAD):
                    pool.indirect_dma_start(gathered_rows[s][:, a, :], None, l.gather_from,
                                            bass.IndirectOffsetOnAxis(ap=gather_now[s][:, a:a + 1], axis=0)
                                            ).then_inc(l.gathered[s], 16)

            def scatter(l, t):
                for a in range(QUAD):
                    pool.indirect_dma_start(l.scatter_to,
                                            bass.IndirectOffsetOnAxis(ap=scatter_now[t.slot(AHEAD)][:, a:a + 1], axis=0),
                                            message[t.slot(2)][:, a, :], None, compute_op=ALU.add
                                            ).then_inc(l.scattered[t.slot(2)], 16)

            def gather_next(l, t):
                pool.wait_ge(l.gather_ready, t.n + 1)
                pool.wait_ge(l.normed_ready, t.n - AHEAD + 1)
                pool.sem_inc(pool_gate, 1)
                gather(l, t)

            def step(l, t):
                pool.wait_ge(l.scatter_ready, t.n + 3)
                pool.wait_ge(l.message_ready, t.n + 3)
                pool.sem_inc(pool_gate, 1)
                scatter(l, t)
                if (t + (AHEAD + 1)).below(GROUPS):
                    gather_next(l, t + (AHEAD + 1))
                pool.wait_ge(l.scattered[t.slot(2)], (t.use(2) + 1) * (16 * QUAD))
                pool.sem_inc(l.retired, 1)

            for l in layers:
                for g in range(AHEAD):
                    pool.wait_ge(l.gather_ready, g + 1)
                    gather(l, Turn(0, 0, g))
                gather_next(l, Turn(0, 0, AHEAD))
                if l.n == 0:
                    for s in range(2):
                        pool.wait_ge(x1_copied[s], 16 * COPY_PIECES // 2)
                    pool.wait_ge(dump_zeroed, 32)
                else:
                    pool.wait_ge(agg_zeroed, 16 * ZERO_PIECES)
                turns(pool, GROUPS, 2, AHEAD + 1, lambda t: step(l, t))

        @block.scalar
        def _(act):
            act.wait_ge(wT_done, 1)
            act.activation(wT_hi[:, :, :].rearrange("p k o -> p (k o)"), ps_a[:, 0, 0:KB * D], ACT.Copy).then_inc(wT_ready, 1)
            for l in layers:
                act.sem_inc(l.message_ready, 2)
                act.sem_inc(l.targets_ready, 1)
            act.wait_ge(consts_ready, 2)

            def take_targets(l, t):
                s = t.slot(2)
                act.wait_ge(l.targets_spread, t.n + 1)
                act.wait_ge(l.same_ready, t.n + 1)
                act.activation(targets_sb[s], ps_a[:, 0, :], ACT.Copy).then_inc(l.targets_ready, 1)

            def std(l, t):
                s = t.slot(2)
                act.wait_ge(l.moments_ready, t.n + 1)
                act.activation(row_std[s][:, :], row_moments[s][:, :, 1], ACT.Sqrt, bias=eps_col[:, :]).then_inc(l.std_ready, 1)

            def norm(l, t):
                s = t.slot(2)
                act.wait_ge(l.norm_ready, t.n + 1)
                if l.n == 0 and t.n_above(1):
                    act.wait_ge(l.rows_lo_ready, t.n + -1)
                if l.n == 1:
                    act.wait_ge(l.message_done, t.n + 1)
                for a in range(QUAD):
                    ins = act.activation(normed[s][:, a, :], gathered_rows[t.slot(AHEAD)][:, a, :], ACT.Relu,
                                         scale=row_norm[s][:, 0, a:a + 1], bias=row_norm[s][:, 1, a:a + 1])
                ins.then_inc(l.normed_ready, 1)

            def weigh(l, t):
                s = t.slot(2)
                act.wait_ge(l.normed_ready, t.n + 1)
                for a in range(QUAD):
                    act.activation(rows_hi[s][:, a, :], normed[s][:, a, :], ACT.Copy,
                                   scale=info_now[t.slot(AHEAD)][:, QUAD + a:QUAD + a + 1]).then_inc(l.rows_hi_ready, 1)

            def take_sums(l, t):
                for kb in range(KB):
                    act.wait_ge(l.summed, t.n * KB + kb + 1)
                    act.activation(summed_hi[:, kb, :], ps_a[:, 2 + kb, :], ACT.Copy).then_inc(l.sums_hi_ready, 1)

            def take_message(l, t):
                s = t.slot(2)
                act.wait_ge(l.message_done, t.n + 3)
                act.wait_ge(l.retired, t.n + AHEAD - 1)
                act.activation(message[s].rearrange("p (u a) d -> p u (a d)", u=2), ps_b[:, 2 * s:2 * s + 2, :],
                               ACT.Copy).then_inc(l.message_ready, 1)

            def edges(l, t):
                if (t + 1).below(GROUPS):
                    take_targets(l, t + 1)
                if (t + -1).below(GROUPS):
                    take_message(l, t + -1)
                if (t + 2).below(GROUPS):
                    std(l, t + 2)
                if l.n == 0 and t.below(GROUPS):
                    take_sums(l, t)
                if l.n == 0 and (t + 1).below(GROUPS):
                    weigh(l, t + 1)
                if (t + 2).below(GROUPS):
                    norm(l, t + 2)

            for l in layers:
                edges(l, Turn(0, 0, -2))
                edges(l, Turn(0, 0, -1))
                turns(act, GROUPS + 1, 1, 3, lambda t: edges(l, t))

            act.wait_ge(stats_done, CHUNKS)
            act.activation(node_std[:, :, :], node_moments[:, :, :, 1], ACT.Sqrt, bias=eps_col[:, :]).then_inc(node_std_ready, 1)

            def relu_norm(c, s, load):
                p, j = shape_of(c)
                for r in range(j):
                    ins = act.activation(relu_ln[s][0:p, r, :], x1_in[load][0:p, r, :], ACT.Relu,
                                         scale=norm_now[s][0:p, 0, r:r + 1], bias=norm_now[s][0:p, 1, r:r + 1])
                return ins

            def gram_norm(t):
                s = t.slot(LOADS)
                act.wait_ge(norm_picked, t.n + 1)
                act.wait_ge(gram_x_loaded[s], t.use(LOADS) * 16 + 16)
                act.wait_ge(gram_h, t.n + LOADS - 1)
                relu_norm(t.n, t.slot(2), s).then_inc(gram_relu, 1)

            def gram(t):
                s = t.slot(2)
                if (t + 1).below(CHUNKS):
                    gram_norm(t + 1)
                act.wait_ge(gram_h, t.n + LOADS + 1)
                act.wait_ge(gram_used, t.n + 1)
                p, j = shape_of(t.n)
                act.activation(gram_in[s][0:p, 0:j, 0, :], h[s][0:p, 0:j, :], ACT.Copy).then_inc(gram_hi, 1)
            gram_norm(Turn(0, 0, 0))
            turns(act, CHUNKS, 0, 4, gram)

            def prepare(n, s, k):
                act.wait_ge(norm_picked, CHUNKS + n + 1)
                act.wait_ge(main_loaded[s], 32 * k + 32)
                relu_norm(n, s % 2, s).then_inc(ln_ready, 1)

            act.wait_ge(gram_used, CHUNKS + 2)
            act.activation(gram0[:, :], ps_a[:, 0, :], ACT.Copy)
            act.activation(gram1[:, :], ps_a[:, 1, 0:D + P], ACT.Copy).then_inc(bn_act, 1)

            prepare(0, 0, 0)
            act.wait_ge(bn_pe, 3 + KB)
            act.activation(bn_std[:, :], ps_b[:, 1, 0:MB], ACT.Sqrt, bias=eps_col[:, :]).then_inc(bn_act, 1)


            def main(n, s, k):
                p, j = shape_of(n)
                w = p * j
                for kb in range(KB):
                    act.wait_ge(hT_done, KB * n + kb + 1)
                    act.activation(hT_hi[:, kb, 0:w], ps_a[:, kb, 0:w], ACT.Copy).then_inc(hT_hi_ready, 1)
                if isinstance(n, int) and n == 0:
                    act.wait_ge(bn_ready, 1)
                for m in range(MB):
                    act.wait_ge(up_done, MB * n + m + 1)
                    if m >= 2:
                        act.wait_ge(hid_lo_ready, MB * n + m - 1)
                    elif not (isinstance(n, int) and n == 0):
                        act.wait_ge(hid_lo_ready, MB * n + m - 1)
                    act.activation(hid[m % 2][:, 0:w], ps_a[:, 2 + m % 2, 0:w], ACT.Relu,
                                   scale=bn_scale[:, m:m + 1], bias=bn_bias[:, m:m + 1]).then_inc(hid_ready, 1)
                    if m >= 4 or not (isinstance(n, int) and n == 0):
                        act.wait_ge(down_done, MB * n + m - 3)
                    act.wait_ge(hid_ready, MB * n + m + 1)
                    act.activation(hid_hi[m % 4][:, 0:w], hid[m % 2][:, 0:w], ACT.Copy).then_inc(hid_hi_ready, 1)
                    if m == 3 and not (isinstance(n, int) and n == CHUNKS - 1):
                        prepare(n + 1, (s + 1) % LOADS, (k if s < LOADS - 1 else k + 1))
            main_schedule(act, main)

        @block.vector
        def _(dve):
            class Chain:
                def __init__(self):
                    self.before, self.n = 0, 0

                def then(self, ins):
                    self.n += 1
                    ins.then_inc(dve_step, 1)
                    return self.n

                def wait(self, number=None):
                    dve.wait_ge(dve_step, self.before + (self.n if number is None else number))

            chain = Chain()

            def looped(count, per, body):
                start = chain.before + chain.n
                with dve.Fori(0, count) as i:
                    chain.before, chain.n = i * per + start, 0
                    body(i)
                    assert chain.n == per, chain.n
                chain.before, chain.n = start + count * per, 0

            dve.wait_ge(ids_loaded, 16 * 10)
            for n in range(2):
                view = lambda t: t[:, :].rearrange("p (g a) -> p g a", a=QUAD)
                chain.then(dve.tensor_copy(edge_info[n][:, :, 0:QUAD], view(target_ids[n])))
                chain.then(dve.tensor_copy(edge_info[n][:, :, QUAD:2 * QUAD], view(weights)))
                chain.then(dve.tensor_copy(edge_info[n][:, :, 2 * QUAD:3 * QUAD], view(dump_ids)))
                chain.wait()
                dve.tensor_tensor(edge_info[n][:, :, 2 * QUAD:3 * QUAD], edge_info[n][:, :, 2 * QUAD:3 * QUAD],
                                  edge_info[n][:, :, 0:QUAD], ALU.subtract).then_inc(info_built, 1)
            dve.wait_ge(info_built, 2)

            def pick_gather(l, t):
                dve.tensor_copy(gather_now[t.slot(AHEAD)][:, :],
                                l.gather_ids[:, bass.ds(t.n * QUAD, QUAD)]).then_inc(l.gather_ready, 1)

            def pick_info(l, t):
                if t.n_above(1):
                    dve.wait_ge(l.scatter_ready, t.n + -1)
                dve.tensor_copy(info_now[t.slot(AHEAD)][:, :],
                                l.info[:, bass.ds(t.n, 1), :].rearrange("p g i -> p (g i)")).then_inc(l.info_ready, 1)

            def row_statistics(l, t):
                dve.wait_ge(l.gathered[t.slot(AHEAD)], (t.use(AHEAD) + 1) * (16 * QUAD))
                for a in range(QUAD):
                    ins = dve.bn_stats(row_stats[:, a, :], gathered_rows[t.slot(AHEAD)][:, a, :])
                return chain.then(ins)

            def row_aggregates(l, t, number):
                chain.wait(number)
                if (t + AHEAD).below(GROUPS):
                    pick_gather(l, t + AHEAD)
                for a in range(QUAD):
                    ins = dve.bn_aggr(row_moments[t.slot(2)][:, a, :], row_stats[:, a, :])
                ins.then_inc(l.moments_ready, 1)

            def row_rstd(l, t):
                dve.wait_ge(l.std_ready, t.n + 1)
                if t.n_above(1):
                    dve.wait_ge(l.normed_ready, t.n + -1)
                return chain.then(dve.reciprocal(row_norm[t.slot(2)][:, 0, :], row_std[t.slot(2)][:, :]))

            def row_shift(l, t, number):
                s = t.slot(2)
                chain.wait(number)
                dve.scalar_tensor_tensor(row_norm[s][:, 1, :], row_moments[s][:, :, 0], -1.0, row_norm[s][:, 0, :],
                                         ALU.mult, ALU.mult).then_inc(l.norm_ready, 1)

            def compare(l, t):
                s, info = t.slot(2), info_now[t.slot(AHEAD)]
                dve.wait_ge(l.targets_ready, t.n + 2)
                dve.wait_ge(l.counted, t.n + 1)
                if l.n == 1:
                    dve.wait_ge(l.message_done, t.n + 1)
                for a in range(QUAD):
                    ins = dve.tensor_scalar(same[s][:, a, :], targets_sb[s], info[:, a:a + 1], None, ALU.is_equal)
                ins.then_inc(l.same_ready, 1)

            def compare_before(l, t):
                s = t.slot(2)
                dve.wait_ge(l.same_ready, t.n + 3)
                dve.tensor_tensor(same_before[s], same_diagonal[s].bitcast(F32),
                                  before[:, :].rearrange("p (a q) -> p a q", a=1).to_broadcast([P, QUAD, P]),
                                  ALU.mult).then_inc(l.before_ready, 1)

            def weigh_low(l, t):
                s, info = t.slot(2), info_now[t.slot(AHEAD)]
                for a in range(QUAD):
                    dve.wait_ge(l.rows_hi_ready, t.n * QUAD + a + 1)
                    ins = dve.scalar_tensor_tensor(rows_lo[s][:, a, :], normed[s][:, a, :], info[:, QUAD + a:QUAD + a + 1],
                                                   rows_hi[s][:, a, :].bitcast(F32), ALU.mult, ALU.subtract)
                ins.then_inc(l.rows_lo_ready, 1)

            def sums_low(l, t, kb):
                dve.wait_ge(l.sums_hi_ready, t.n * KB + kb + 1)
                dve.tensor_tensor(summed_lo[:, kb, :], ps_a[:, 2 + kb, :], summed_hi[:, kb, :].bitcast(F32),
                                  ALU.subtract).then_inc(l.sums_lo_ready, 1)

            def dump_shift(l, t):
                dve.wait_ge(l.counted, t.n + 3)
                return chain.then(dve.scalar_tensor_tensor(
                    shift[:, :], counts, 0.0, info_now[t.slot(AHEAD)][:, 2 * QUAD:3 * QUAD], ALU.is_gt, ALU.mult))

            def scatter_rows(l, t, number):
                chain.wait(number)
                dve.wait_ge(l.retired, t.n + 1)
                dve.tensor_tensor(scatter_now[t.slot(AHEAD)][:, :], shift[:, :], info_now[t.slot(AHEAD)][:, 0:QUAD],
                                  ALU.add).then_inc(l.scatter_ready, 1)

            def node_statistics(c, s, k):
                p, j = shape_of(c)
                dve.wait_ge(stats_loaded[s], 16 * k + 16)
                for r in range(j):
                    ins = dve.bn_stats(node_stats[s][0:p, r, :], x1_in[s][0:p, r, :])
                return chain.then(ins)

            def node_aggregates(c, s, number):
                p, j = shape_of(c)
                chain.wait(number)
                dve.sem_inc(stats_taken, 1)
                for r in range(j):
                    ins = dve.bn_aggr(chunk_moments[s][0:p, r, :], node_stats[s][0:p, r, :])
                return chain.then(ins)

            def keep_aggregates(c, s, number):
                p, j = shape_of(c)
                chain.wait(number)
                dve.tensor_copy(node_moments[0:p, bass.ds(c, 1), 0:j, :].rearrange("p c j t -> p (c j t)"),
                                chunk_moments[s][0:p, 0:j, :].rearrange("p j t -> p (j t)")).then_inc(stats_done, 1)

            def edge_step(l, t):
                here, next1, next2 = (u.below(GROUPS) for u in (t, t + 1, t + 2))
                sums, nodes = here and l.n == 0, here and l.n == 1
                if (t + 3).below(GROUPS):
                    pick_info(l, t + 3)
                if next2:
                    rows = row_statistics(l, t + 2)
                if nodes:
                    nodes0 = node_statistics(t.n * 2, 0, t.n)
                if next1 and l.n == 0:
                    compare(l, t + 1)
                if next2:
                    row_aggregates(l, t + 2, rows)
                if next1 and l.n == 1:
                    compare(l, t + 1)
                if nodes:
                    nodes0 = node_aggregates(t.n * 2, 0, nodes0)
                if next1:
                    compare_before(l, t + 1)
                if nodes:
                    nodes1 = node_statistics(t.n * 2 + 1, 1, t.n)
                if sums:
                    sums_low(l, t, 0)
                if next2:
                    rstd = row_rstd(l, t + 2)
                if nodes:
                    keep_aggregates(t.n * 2, 0, nodes0)
                if sums:
                    sums_low(l, t, 1)
                if here:
                    moved = dump_shift(l, t)
                if nodes:
                    nodes1 = node_aggregates(t.n * 2 + 1, 1, nodes1)
                if next2:
                    row_shift(l, t + 2, rstd)
                if here:
                    scatter_rows(l, t, moved)
                if l.n == 0 and next1:
                    weigh_low(l, t + 1)
                if nodes:
                    keep_aggregates(t.n * 2 + 1, 1, nodes1)

            dve.sem_inc(stats_taken, 2)
            dve.sem_inc(gram_h, LOADS)
            for l in layers:
                dve.sem_inc(l.same_ready, 2)
                dve.sem_inc(l.scatter_ready, 2)
            dve.sem_inc(gram_lo, 2)
            dve.wait_ge(consts_ready, 3)
            chain.then(dve.tensor_copy(ones_r[:, :], ones[:, :]))

            dve.wait_ge(wT_ready, 1)
            dve.tensor_tensor(wT_lo[:, :, :].rearrange("p k o -> p (k o)"), ps_a[:, 0, 0:KB * D],
                              wT_hi[:, :, :].rearrange("p k o -> p (k o)").bitcast(F32), ALU.subtract).then_inc(wT_ready, 1)

            EDGE = 3
            NODE = 4
            for l in layers:
                for g in range(AHEAD):
                    pick_gather(l, Turn(0, 0, g))
                if l.n == 1:
                    dve.wait_ge(layers[0].scatter_ready, GROUPS + 2)
                pick_info(l, Turn(0, 0, 0))
                if l.n == 1:
                    dve.wait_ge(w12_loaded, 16 * 6)
                    chain.then(dve.tensor_copy(w1_hi[:, :, :], w1_f[:, :, :]))
                    chain.then(dve.tensor_copy(w2_hl[:, :, 0, :], w2_f[:, :, :]))
                    chain.wait()
                    dve.tensor_tensor(w1_lo[:, :, :], w1_f[:, :, :], w1_hi[:, :, :].bitcast(F32), ALU.subtract)
                    dve.tensor_tensor(w2_hl[:, :, 1, :], w2_f[:, :, :], w2_hl[:, :, 0, :].bitcast(F32),
                                      ALU.subtract).then_inc(w12_split, 1)
                    dve.wait_ge(layers[0].retired, GROUPS + AHEAD)
                edge_step(l, Turn(0, 0, -2))
                edge_step(l, Turn(0, 0, -1))
                turns(dve, GROUPS, 1, AHEAD + 2, lambda t: edge_step(l, t),
                      loop=lambda passes, body: looped(passes, AHEAD * (EDGE + NODE * l.n), body))

            dve.wait_ge(node_std_ready, 1)
            chain.then(dve.reciprocal(node_rstd[:, :, :], node_std[:, :, :]))
            chain.wait()
            chain.then(dve.scalar_tensor_tensor(node_shift[:, :, :], node_moments[:, :, :, 0], -1.0, node_rstd[:, :, :],
                                                ALU.mult, ALU.mult))
            chain.wait()

            def pick_norm(c, s):
                dve.tensor_copy(norm_now[s][:, 0, :], node_rstd[:, bass.ds(c, 1), :].rearrange("p c j -> p (c j)"))
                dve.tensor_copy(norm_now[s][:, 1, :], node_shift[:, bass.ds(c, 1), :].rearrange("p c j -> p (c j)")).then_inc(norm_picked, 1)

            pick_norm(0, 0)
            pick_norm(1, 1)

            def gram_add(t):
                s, p, j = t.slot(2), *shape_of(t.n)
                dve.wait_ge(gram_relu, t.n + 1)
                dve.wait_ge(gram_a_loaded[t.slot(LOADS)], t.use(LOADS) * 16 + 16)
                dve.wait_ge(gram_lo, t.n + 1)
                dve.tensor_tensor(h[s][0:p, 0:j, :], relu_ln[s][0:p, 0:j, :], agg_in[t.slot(LOADS)][0:p, 0:j, :],
                                  ALU.add).then_inc(gram_h, 1)
                if (t + 2).below(CHUNKS):
                    pick_norm(t.n + 2, s)

            def gram(t):
                s, p, j = t.slot(2), *shape_of(t.n)
                if (t + 1).below(CHUNKS):
                    gram_add(t + 1)
                dve.wait_ge(gram_hi, t.n + 1)
                dve.tensor_tensor(gram_in[s][0:p, 0:j, 1, :], h[s][0:p, 0:j, :], gram_in[s][0:p, 0:j, 0, :].bitcast(F32),
                                  ALU.subtract).then_inc(gram_lo, 1)
            gram_add(Turn(0, 0, 0))
            turns(dve, CHUNKS, 0, 4, gram)
            pick_norm(0, 0)
            pick_norm(1, 1)

            def add_agg(n, s, k):
                p, j = shape_of(n)
                dve.wait_ge(ln_ready, n + 1)
                dve.wait_ge(main_loaded[s], 32 * k + 32)
                dve.tensor_tensor(h[s % 2][0:p, 0:j, :], relu_ln[s % 2][0:p, 0:j, :], agg_in[s][0:p, 0:j, :], ALU.add).then_inc(h_ready, 1)

            dve.wait_ge(gram_used, CHUNKS + 2)
            chain.then(dve.tensor_scalar(gram_sum[:, :], ps_a[:, 2, 0:D], 1.0 / N, None, ALU.mult))
            chain.wait()
            dve.scalar_tensor_tensor(mu_row[:, :], ps_a[:, 2, D:2 * D], 1.0 / N, gram_sum[:, :], ALU.mult,
                                     ALU.add).then_inc(bn_act, 1)
            dve.wait_ge(bn_act, 2)
            chain.then(dve.tensor_tensor(cov[0][:, :], gram0[:, 0:D], gram0[:, D:2 * D], ALU.add))
            chain.then(dve.tensor_tensor(cov[1][:, P:D], gram1[:, 0:P], gram1[:, D:D + P], ALU.add))
            dve.wait_ge(bn_pe, 1)
            chain.wait()
            chain.then(dve.tensor_tensor(cov[0][:, :], cov[0][:, :], ps_b[:, 0, 0:D], ALU.add))
            chain.then(dve.tensor_tensor(cov[1][:, P:D], cov[1][:, P:D], ps_b[:, 0, D:D + P], ALU.add))
            chain.then(dve.tensor_scalar(mu_col[:, :], ps_b[:, 3, 0:KB], 1.0 / P, None, ALU.mult))
            chain.wait()
            chain.then(dve.scalar_tensor_tensor(cov[0][:, :], cov[0][:, :], 1.0 / N, ps_b[:, 1, 0:D], ALU.mult, ALU.subtract))
            dve.scalar_tensor_tensor(cov[1][:, P:D], cov[1][:, P:D], 1.0 / N, ps_b[:, 2, P:D], ALU.mult,
                                     ALU.subtract).then_inc(bn_act, 1)
            dve.wait_ge(bn_pe, 2)
            dve.tensor_copy(cov[1][:, 0:P], ps_b[:, 0, 0:P]).then_inc(bn_act, 1)
            add_agg(0, 0, 0)
            for i in range(KB):
                dve.wait_ge(bn_pe, 3 + i)
                dve.tensor_tensor(w1_cov[:, i, :].rearrange("p (a n) -> p a n", a=2),
                                  w1_f[:, i, :].rearrange("p (a n) -> p a n", a=2),
                                  ps_a[:, 2 * i:2 * i + 2, :], ALU.mult).then_inc(bn_act, 1)
            dve.wait_ge(bn_pe, 3 + KB)
            chain.then(dve.tensor_tensor(bn_mean[:, :], ps_b[:, 2, 0:MB], b1_v, ALU.add))
            dve.wait_ge(bn_act, 5 + KB)
            chain.then(dve.reciprocal(bn_scale[:, :], bn_std[:, :]))
            chain.wait()
            chain.then(dve.tensor_tensor(bn_scale[:, :], bn_scale[:, :], gamma_v, ALU.mult))
            chain.then(dve.tensor_tensor(bn_mean[:, :], b1_v, bn_mean[:, :], ALU.subtract))
            chain.wait()
            chain.then(dve.tensor_tensor(bn_bias[:, :], bn_scale[:, :], bn_mean[:, :], ALU.mult))
            chain.wait()
            dve.tensor_tensor(bn_bias[:, :], bn_bias[:, :], beta_v, ALU.add).then_inc(bn_ready, 1)

            def read_down(n, s):
                p, j = shape_of(n)
                dve.wait_ge(out_retired, n + 1)
                for half, rows in enumerate(halves(j)):
                    if half == 0:
                        dve.wait_ge(down_half, n + 1)
                    else:
                        dve.wait_ge(down_done, MB * n + MB)
                    r0, r1 = rows[0], rows[-1] + 1
                    chain.then(dve.tensor_tensor(out_sb[s][0:p, r0:r1, :], ps_b[0:p, r0:r1, 0:D],
                                                 b2_bc[0:p, :].rearrange("p (a d) -> p a d", a=1).to_broadcast([p, r1 - r0, D]), ALU.add))
                    chain.wait()
                    dve.tensor_tensor(out_sb[s][0:p, r0:r1, :], out_sb[s][0:p, r0:r1, :], ps_b[0:p, r0:r1, D:2 * D],
                                      ALU.add).then_inc(down_read, 1)

            def finish(n, s):
                p, j = shape_of(n)
                dve.wait_ge(down_read, 2 * n + 2)
                dve.scalar_tensor_tensor(out_sb[s % 2][0:p, 0:j, :], out_sb[s % 2][0:p, 0:j, :], 0.0, x1_in[s][0:p, 0:j, :],
                                         ALU.max, ALU.add).then_inc(out_ready, 1)

            def main(n, s, k):
                p, j = shape_of(n)
                w = p * j
                first = isinstance(n, int) and n == 0
                for kb in range(KB):
                    dve.wait_ge(hT_hi_ready, KB * n + kb + 1)
                    dve.tensor_tensor(hT_lo[:, kb, 0:w], ps_a[:, kb, 0:w], hT_hi[:, kb, 0:w].bitcast(F32),
                                      ALU.subtract).then_inc(hT_lo_ready, 1)
                if not first:
                    read_down(n - 1, 1 - s % 2)
                for m in range(MB):
                    dve.wait_ge(hid_hi_ready, MB * n + m + 1)
                    if m >= 4 or not first:
                        dve.wait_ge(down_done, MB * n + m - 3)
                    dve.tensor_tensor(hid_lo[m % 4][:, 0:w], hid[m % 2][:, 0:w], hid_hi[m % 4][:, 0:w].bitcast(F32),
                                      ALU.subtract).then_inc(hid_lo_ready, 1)
                    if m == 1 and not first:
                        finish(n - 1, (s - 1) % LOADS)
                    if m == 5 and not (isinstance(n, int) and n == CHUNKS - 1):
                        add_agg(n + 1, (s + 1) % LOADS, (k if s < LOADS - 1 else k + 1))
                    if m == 2 and not (isinstance(n, int) and n + 2 >= CHUNKS):
                        pick_norm(n + 2, s % 2)
            main_schedule(dve, main, loop=lambda passes, body: looped(passes, 2 * LOADS, body))
            read_down(CHUNKS - 1, (CHUNKS - 1) % 2)
            finish(CHUNKS - 1, (CHUNKS - 1) % LOADS)

        @block.tensor
        def _(pe):
            for l in layers:
                pe.sem_inc(l.message_done, 2)
                pe.sem_inc(l.counted, 2)
            pe.sem_inc(gram_used, 2)
            pe.wait_ge(consts_ready, 3)
            pe.wait_ge(w_loaded, 16)
            for k in range(KB):
                for o in range(KB):
                    ins = pe.transpose(ps_a[:, 0, k * D + o * P:k * D + (o + 1) * P], w_rows[:, o, k * P:(k + 1) * P], ident[:, :])
            ins.then_inc(wT_done, 1)
            pe.wait_ge(wT_ready, 2)

            def spread(l, t):
                pe.wait_ge(l.info_ready, t.n + 1)
                pe.wait_ge(l.targets_ready, t.n + 1)
                for b in range(QUAD):
                    ins = pe.transpose(ps_a[:, 0, b * P:(b + 1) * P],
                                       info_now[t.slot(AHEAD)][:, b:b + 1].to_broadcast([P, P]), ident[:, :])
                ins.then_inc(l.targets_spread, 1)

            def sum_rows(l, t):
                s = t.slot(2)
                pe.wait_ge(l.same_ready, t.n + 3)
                pe.wait_ge(l.rows_lo_ready, t.n + 1)
                for kb in range(KB):
                    for a in range(QUAD):
                        for part in (rows_hi[s], rows_lo[s]):
                            ins = pe.matmul(ps_a[:, 2 + kb, :], part[:, a, kb * P:(kb + 1) * P], same[s][:, a, :],
                                            start=(a == 0 and part is rows_hi[s]), stop=(a == QUAD - 1 and part is rows_lo[s]))
                    ins.then_inc(l.summed, 1)

            def count(l, t):
                s = t.slot(2)
                pe.wait_ge(l.before_ready, t.n + 1)
                pe.wait_ge(l.scatter_ready, t.n + 2)
                for b in range(QUAD):
                    for a in range(b + 1):
                        block = same[s][:, a, b * P:(b + 1) * P] if a < b else same_before[s][:, a, :]
                        ins = pe.matmul(ps_a[:, 1, 2 * b:2 * b + 2], block, ones_r[:, 0:2],
                                        start=(a == 0), stop=(a == b))
                ins.then_inc(l.counted, 1)

            def multiply(l, t):
                s = t.slot(2)
                pe.wait_ge(l.sums_lo_ready, t.n * KB + KB)
                pe.wait_ge(l.message_ready, t.n + 1)
                terms = [(sums, weight, kb) for kb in range(KB)
                         for sums, weight in ((summed_hi, wT_hi), (summed_hi, wT_lo), (summed_lo, wT_hi))]
                for b in range(QUAD):
                    for i, (sums, weight, kb) in enumerate(terms):
                        ins = pe.matmul(ps_b[:, 2 * s + b // 2, b % 2 * D:(b % 2 + 1) * D], sums[:, kb, b * P:(b + 1) * P],
                                        weight[:, kb, :], start=(i == 0), stop=(i == len(terms) - 1))
                ins.then_inc(l.message_done, 1)

            def sum_messages(l, t):
                s = t.slot(2)
                pe.wait_ge(l.same_ready, t.n + 3)
                pe.wait_ge(l.normed_ready, t.n + 1)
                pe.wait_ge(l.message_ready, t.n + 1)
                for b in range(QUAD):
                    for a in range(QUAD):
                        ins = pe.matmul(ps_b[:, 2 * s + b // 2, b % 2 * D:(b % 2 + 1) * D],
                                        same[s][:, a, b * P:(b + 1) * P].bitcast(F32), normed[s][:, a, :],
                                        start=(a == 0), stop=(a == QUAD - 1))
                ins.then_inc(l.message_done, 1)

            def edges(l, t):
                if l.n == 0:
                    sum_rows(l, t)
                else:
                    count(l, t)
                    sum_messages(l, t)
                if (t + 2).below(GROUPS):
                    spread(l, t + 2)
                if l.n == 0:
                    count(l, t)
                    multiply(l, t)

            for l in layers:
                spread(l, Turn(0, 0, 0))
                spread(l, Turn(0, 0, 1))
                turns(pe, GROUPS, 1, 2, lambda t: edges(l, t))

            def gram(t):
                s, p, j = t.slot(2), *shape_of(t.n)
                pe.wait_ge(gram_lo, t.n + 3)
                for r in range(j):
                    first = not t.per and t.n == 0 and r == 0
                    last = not t.per and t.n == CHUNKS - 1 and r == j - 1
                    both = gram_in[s][0:p, r, :, :].rearrange("p t d -> p (t d)")
                    pe.matmul(ps_a[:, 0, :], both[:, 0:P], both, start=first, stop=last)
                    pe.matmul(ps_a[:, 1, 0:D + P], both[:, P:D], both[:, P:2 * D], start=first, stop=last)
                    ins = pe.matmul(ps_a[:, 2, :], ones_r[0:p, :], both, start=first, stop=last)
                ins.then_inc(gram_used, 1)
            turns(pe, CHUNKS, 2, 4, gram)

            pe.wait_ge(bn_act, 2)
            pe.transpose(ps_b[:, 0, 0:P], gram0[:, D:D + P], ident[:, :])
            pe.transpose(ps_b[:, 0, P:D], gram1[:, P:D], ident[:, :])
            pe.transpose(ps_b[:, 0, D:D + P], gram1[:, D:D + P], ident[:, :])
            for k in range(KB):
                pe.matmul(ps_b[:, 1 + k, 0:D], mu_row[0:1, k * P:(k + 1) * P], mu_row[0:1, :], start=True, stop=True)
            for k in range(KB):
                ins = pe.matmul(ps_b[:, 3, k:k + 1], mu_row[:, k * P:(k + 1) * P], ones[:, 0:1], start=True, stop=True)
            ins.then_inc(bn_pe, 1)
            pe.wait_ge(bn_act, 3)
            pe.transpose(ps_b[:, 0, 0:P], cov[0][:, P:D], ident[:, :]).then_inc(bn_pe, 1)
            pe.wait_ge(bn_act, 4)
            for i in range(KB):
                for a in range(2):
                    for k in range(KB):
                        ins = pe.matmul(ps_a[:, 2 * i + a, :], cov[k][:, i * P:(i + 1) * P], w1_f[:, k, a * 512:(a + 1) * 512],
                                        start=(k == 0), stop=(k == KB - 1))
                ins.then_inc(bn_pe, 1)
            for m in range(MB):
                for k in range(KB):
                    ins = pe.matmul(ps_b[:, 2, m:m + 1], w1_f[:, k, m * P:(m + 1) * P], mu_col[:, k:k + 1],
                                    start=(k == 0), stop=(k == KB - 1))
            pe.wait_ge(bn_act, 4 + KB)
            for m in range(MB):
                for i in range(KB):
                    ins = pe.matmul(ps_b[:, 1, m:m + 1], w1_cov[:, i, m * P:(m + 1) * P], ones[:, 0:1],
                                    start=(i == 0), stop=(i == KB - 1))
            ins.then_inc(bn_pe, 1)
            pe.wait_ge(w12_split, 1)

            def transpose_h(n, s):
                p, j = shape_of(n)
                pe.wait_ge(h_ready, n + 1)
                for kb in range(KB):
                    for r in range(j):
                        ins = pe.transpose(ps_a[:, kb, r * p:(r + 1) * p], h[s % 2][0:p, r, kb * P:(kb + 1) * P], ident[0:p, 0:p])
                    ins.then_inc(hT_done, 1)

            def up(n, m):
                p, j = shape_of(n)
                w = p * j
                if m == 0:
                    pe.wait_ge(hT_hi_ready, KB * n + KB)
                    pe.wait_ge(hT_lo_ready, KB * n + KB)
                if m >= 2 or not (isinstance(n, int) and n == 0):
                    pe.wait_ge(hid_ready, MB * n + m - 1)
                cols = slice(m * P, (m + 1) * P)
                terms = [(w_part, h_part, kb) for kb in range(KB)
                         for w_part, h_part in ((w1_hi, hT_hi), (w1_hi, hT_lo), (w1_lo, hT_hi))]
                for t, (w_part, h_part, kb) in enumerate(terms):
                    ins = pe.matmul(ps_a[:, 2 + m % 2, 0:w], w_part[:, kb, cols], h_part[:, kb, 0:w],
                                    start=(t == 0), stop=(t == len(terms) - 1))
                ins.then_inc(up_done, 1)

            def down(n, m, half=None):
                p, j = shape_of(n)
                pe.wait_ge(hid_hi_ready, MB * n + m + 1)
                pe.wait_ge(hid_lo_ready, MB * n + m + 1)
                if m == 0 and not (isinstance(n, int) and n == 0):
                    pe.wait_ge(down_read, 2 * n)
                w2 = w2_hl[:, m, :, :].rearrange("p t d -> p (t d)")
                for r in (range(j) if half is None else halves(j)[half]):
                    cols = slice(r * p, (r + 1) * p)
                    pe.matmul(ps_b[0:p, r, :], hid_hi[m % 4][:, cols], w2, start=(m == 0), stop=(m == MB - 1), skip_group_check=True)
                    ins = pe.matmul(ps_b[0:p, r, 0:D], hid_lo[m % 4][:, cols], w2[:, 0:D], start=False, stop=(m == MB - 1), skip_group_check=True)
                ins.then_inc(down_half if half == 0 else down_done, 1)

            def main(n, s, k):
                transpose_h(n, s)
                if not (isinstance(n, int) and n == 0):
                    down(n - 1, MB - 2)
                    down(n - 1, MB - 1, half=0)
                up(n, 0)
                if not (isinstance(n, int) and n == 0):
                    down(n - 1, MB - 1, half=1)
                up(n, 1)
                for m in range(2, MB):
                    up(n, m)
                    down(n, m - 2)
            main_schedule(pe, main)
            down(CHUNKS - 1, MB - 2)
            down(CHUNKS - 1, MB - 1, half=0)
            down(CHUNKS - 1, MB - 1, half=1)


def kernel(x, src, dst, edge_weight, L0_gnn_W, L1_gnn_W1, L1_gnn_b1, L1_gnn_gamma, L1_gnn_beta, L1_gnn_W2, L1_gnn_b2):
    import numpy as np
    import concourse.bacc as bacc
    from concourse import mybir
    from concourse.bass_utils import run_bass_kernel_spmd

    nc = bacc.Bacc("TRN2", target_bir_lowering=False, num_devices=1)
    given = dict(x=x, src=src, dst=dst, edge_weight=edge_weight, W=L0_gnn_W, W1=L1_gnn_W1, b1=L1_gnn_b1,
                 gamma=L1_gnn_gamma, beta=L1_gnn_beta, W2=L1_gnn_W2, b2=L1_gnn_b2)
    arrays = {f"in_{name}": np.ascontiguousarray(a) for name, a in given.items()}
    aps = {name: nc.dram_tensor(f"in_{name}", arrays[f"in_{name}"].shape,
                                mybir.dt.from_np(arrays[f"in_{name}"].dtype), kind="ExternalInput").ap()
           for name in given}
    out = nc.dram_tensor("out", arrays["in_x"].shape, mybir.dt.float32, kind="ExternalOutput").ap()
    gnn_program(nc, out=out, **aps)
    result = run_bass_kernel_spmd(nc, [arrays], core_ids=[0])
    return result.results[0]["out"]
```
